# Optimizing a Trainium2 kernel written in Bass

```python
import numpy as np
import jax
import jax.numpy as jnp

def _softmax(x, axis=-1):
    return jax.nn.softmax(x, axis=axis)

def _gelu(x):
    return jax.nn.gelu(x, approximate=True)

def _silu(x):
    return jax.nn.silu(x)

def _sigmoid(x):
    return jax.nn.sigmoid(x)

def _layernorm(x, axis=-1, eps=1e-05):
    m = jnp.mean(x, axis=axis, keepdims=True)
    v = jnp.var(x, axis=axis, keepdims=True)
    return (x - m) / jnp.sqrt(v + eps)

def _scatter_add(tgt, idx, src, axis=0):
    return tgt.at[idx].add(src)

def _segment_sum(src, seg, n):
    return jax.ops.segment_sum(src, seg, n)
kernel_name = 'mk_gnn_preln_d2_gnn_r32_505172'

def setup_inputs(seed: int=0):
    np.random.seed(seed)
    _w = jnp.asarray

    def _rec_inputs():
        import jax
        import jax.numpy as jnp
        _gk = jax.random.key(seed)
        x = -0.0006008 + 1.001 * jax.random.normal(jax.random.fold_in(_gk, 1), (3125, 256), jnp.float32)
        src = jax.random.randint(jax.random.fold_in(_gk, 2), (50000,), 0, 3125, jnp.int32)
        dst = jnp.minimum((3125 * jax.random.uniform(jax.random.fold_in(_gk, 3), (50000,)) ** 2.0).astype(jnp.int32), 99999)
        _o = jnp.argsort(dst, stable=True)
        src = src[_o]
        dst = dst[_o]
        edge_attr_16 = 0.000130101 + 1.00012 * jax.random.normal(jax.random.fold_in(_gk, 12), (50000, 16), jnp.float32)
        return (x, src, dst, edge_attr_16)
    x, src, dst, edge_attr_16 = _rec_inputs()

    def _L0_gnn_setup():
        import jax, jax.numpy as jnp
        import numpy as np
        N, NODE_DIM, EDGE_DIM, HIDDEN, E = (10000, 256, 16, 512, 10000)
        key = jax.random.key(seed)
        ks = jax.random.split(key, 12)

        def lin(kw, kb, fan_in, fan_out):
            bound = 1.0 / np.sqrt(fan_in)
            W = jax.random.uniform(kw, (fan_in, fan_out), jnp.float32, -bound, bound)
            b = jax.random.uniform(kb, (fan_out,), jnp.float32, -bound, bound)
            return (W, b)
        node_features = jax.random.normal(ks[0], (N, NODE_DIM), jnp.float32)
        edge_index = jax.random.randint(ks[1], (2, E), 0, N, jnp.int32)
        edge_features = jax.random.normal(ks[2], (E, EDGE_DIM), jnp.float32)
        mW1, mb1 = lin(ks[3], ks[4], 2 * NODE_DIM + EDGE_DIM, HIDDEN)
        mW2, mb2 = lin(ks[5], ks[6], HIDDEN, NODE_DIM)
        uW1, ub1 = lin(ks[7], ks[8], 2 * NODE_DIM, HIDDEN)
        uW2, ub2 = lin(ks[9], ks[10], HIDDEN, NODE_DIM)
        return {'node_features': node_features, 'edge_index': edge_index, 'edge_features': edge_features, 'mW1': mW1, 'mb1': mb1, 'mW2': mW2, 'mb2': mb2, 'uW1': uW1, 'ub1': ub1, 'uW2': uW2, 'ub2': ub2}
    _L0_gnn_all = _L0_gnn_setup()
    _L0_gnn_in = {k: v for k, v in _L0_gnn_all.items() if k in ('mW1', 'mb1', 'mW2', 'mb2', 'uW1', 'ub1', 'uW2', 'ub2')}
    del _L0_gnn_all

    def _L1_gnn_setup():
        import jax, jax.numpy as jnp
        import numpy as np
        N, E = (50000, 25000)
        IN_C, HID_C, OUT_C = (256, 256, 256)

        def _gcn_prep(edge_index, n_nodes):
            src = jnp.concatenate([edge_index[0], jnp.arange(n_nodes, dtype=edge_index.dtype)])
            dst = jnp.concatenate([edge_index[1], jnp.arange(n_nodes, dtype=edge_index.dtype)])
            deg = jax.ops.segment_sum(jnp.ones_like(dst, dtype=jnp.float32), dst, num_segments=n_nodes)
            deg_inv_sqrt = jnp.where(deg > 0, jax.lax.rsqrt(jnp.maximum(deg, 1.0)), 0.0)
            norm = deg_inv_sqrt[src] * deg_inv_sqrt[dst]
            return (src, dst, norm)

        def _gcn_layer(x, src, dst, norm, W, b, n_nodes):
            h = x @ W
            msg = h[src] * norm[:, None]
            out = jax.ops.segment_sum(msg, dst, num_segments=n_nodes)
            return out + b
        key = jax.random.key(seed)
        ks = jax.random.split(key, 8)
        x_piece = jax.random.normal(ks[0], (N, IN_C), dtype=jnp.float32)
        edge_index_piece = jax.random.randint(ks[1], (2, E), 0, N, dtype=jnp.int64)
        batch = jnp.zeros((N,), dtype=jnp.int64)

        def glorot(k, fan_in, fan_out):
            s = jnp.sqrt(6.0 / (fan_in + fan_out)).astype(jnp.float32)
            return jax.random.uniform(k, (fan_in, fan_out), jnp.float32, -s, s)
        return {'x_piece': x_piece, 'edge_index_piece': edge_index_piece, 'batch': batch, 'W1': glorot(ks[2], IN_C, HID_C), 'b1': jnp.zeros((HID_C,), jnp.float32), 'W2': glorot(ks[3], HID_C, HID_C), 'b2': jnp.zeros((HID_C,), jnp.float32), 'W3': glorot(ks[4], HID_C, OUT_C), 'b3': jnp.zeros((OUT_C,), jnp.float32)}
    _L1_gnn_all = _L1_gnn_setup()
    _L1_gnn_in = {k: v for k, v in _L1_gnn_all.items() if k in ('W1', 'b1', 'W2', 'b2', 'W3', 'b3')}
    del _L1_gnn_all
    return {'x': x, 'src': src, 'dst': dst, 'edge_attr_16': edge_attr_16, 'L0_gnn_mW1': _L0_gnn_in['mW1'], 'L0_gnn_mb1': _L0_gnn_in['mb1'], 'L0_gnn_mW2': _L0_gnn_in['mW2'], 'L0_gnn_mb2': _L0_gnn_in['mb2'], 'L0_gnn_uW1': _L0_gnn_in['uW1'], 'L0_gnn_ub1': _L0_gnn_in['ub1'], 'L0_gnn_uW2': _L0_gnn_in['uW2'], 'L0_gnn_ub2': _L0_gnn_in['ub2'], 'L1_gnn_W1': _L1_gnn_in['W1'], 'L1_gnn_b1': _L1_gnn_in['b1'], 'L1_gnn_W2': _L1_gnn_in['W2'], 'L1_gnn_b2': _L1_gnn_in['b2'], 'L1_gnn_W3': _L1_gnn_in['W3'], 'L1_gnn_b3': _L1_gnn_in['b3']}

def reference(x, src, dst, edge_attr_16, L0_gnn_mW1, L0_gnn_mb1, L0_gnn_mW2, L0_gnn_mb2, L0_gnn_uW1, L0_gnn_ub1, L0_gnn_uW2, L0_gnn_ub2, L1_gnn_W1, L1_gnn_b1, L1_gnn_W2, L1_gnn_b2, L1_gnn_W3, L1_gnn_b3):
    import jax
    import jax.numpy as jnp

    def _L0_gnn_ref(node_features, edge_index, edge_features, mW1, mb1, mW2, mb2, uW1, ub1, uW2, ub2):
        import jax, jax.numpy as jnp
        import numpy as np
        N, NODE_DIM, EDGE_DIM, HIDDEN, E = (10000, 256, 16, 512, 10000)
        i_idx = edge_index[0]
        j_idx = edge_index[1]
        node_i = node_features[i_idx]
        node_j = node_features[j_idx]
        msg_input = jnp.concatenate([node_i, node_j, edge_features], axis=-1)
        h = jax.nn.relu(msg_input @ mW1 + mb1)
        messages = h @ mW2 + mb2
        aggregated = jax.ops.segment_sum(messages, i_idx, num_segments=node_features.shape[0])
        update_input = jnp.concatenate([node_features, aggregated], axis=-1)
        u = jax.nn.relu(update_input @ uW1 + ub1)
        updated = u @ uW2 + ub2
        return node_features + updated

    def _L1_gnn_ref(x_piece, edge_index_piece, batch, W1, b1, W2, b2, W3, b3):
        import jax, jax.numpy as jnp
        import numpy as np
        N, E = (50000, 25000)
        IN_C, HID_C, OUT_C = (256, 256, 256)

        def _gcn_prep(edge_index, n_nodes):
            src = jnp.concatenate([edge_index[0], jnp.arange(n_nodes, dtype=edge_index.dtype)])
            dst = jnp.concatenate([edge_index[1], jnp.arange(n_nodes, dtype=edge_index.dtype)])
            deg = jax.ops.segment_sum(jnp.ones_like(dst, dtype=jnp.float32), dst, num_segments=n_nodes)
            deg_inv_sqrt = jnp.where(deg > 0, jax.lax.rsqrt(jnp.maximum(deg, 1.0)), 0.0)
            norm = deg_inv_sqrt[src] * deg_inv_sqrt[dst]
            return (src, dst, norm)

        def _gcn_layer(x, src, dst, norm, W, b, n_nodes):
            h = x @ W
            msg = h[src] * norm[:, None]
            out = jax.ops.segment_sum(msg, dst, num_segments=n_nodes)
            return out + b
        n_nodes = x_piece.shape[0]
        src, dst, norm = _gcn_prep(edge_index_piece, n_nodes)
        x = _gcn_layer(x_piece, src, dst, norm, W1, b1, n_nodes)
        x = jax.nn.gelu(x)
        x = _gcn_layer(x, src, dst, norm, W2, b2, n_nodes)
        x = jax.nn.gelu(x)
        x = _gcn_layer(x, src, dst, norm, W3, b3, n_nodes)
        return x
    edge_index = jnp.stack([src, dst])
    batch0 = jnp.zeros((3125,), jnp.int32)
    h = jnp.maximum(_layernorm(x, axis=-1), 0.0)
    x = x + _L0_gnn_ref(h, edge_index, edge_attr_16, L0_gnn_mW1, L0_gnn_mb1, L0_gnn_mW2, L0_gnn_mb2, L0_gnn_uW1, L0_gnn_ub1, L0_gnn_uW2, L0_gnn_ub2)
    h = jnp.maximum(_layernorm(x, axis=-1), 0.0)
    x = x + _L1_gnn_ref(h, edge_index, batch0, L1_gnn_W1, L1_gnn_b1, L1_gnn_W2, L1_gnn_b2, L1_gnn_W3, L1_gnn_b3)
    return x

_drawn_inputs = setup_inputs


def setup_inputs(seed=0):
    import zlib

    import numpy as np

    out = dict(_drawn_inputs(seed))
    spreads = {'L1_gnn_b1': (0.0, 0.342), 'L1_gnn_b2': (0.0, 0.1), 'L1_gnn_b3': (0.0, 0.1)}
    factors = {'edge_attr_16': 3.519, 'L0_gnn_mb1': 4.29, 'L0_gnn_ub1': 8.0, 'L0_gnn_ub2': 3.463}
    for name, (base, spread) in spreads.items():
        noise = np.random.default_rng([zlib.crc32(name.encode()), seed]).standard_normal(out[name].shape)
        drawn = base * np.exp(spread * noise) if base else spread * noise
        out[name] = jnp.asarray(drawn.astype(out[name].dtype))
    for name, factor in factors.items():
        out[name] = (out[name] * factor).astype(out[name].dtype)
    return out
```

```python
from contextlib import ExitStack

import concourse.bass as bass
from concourse import mybir

P = 128
ALU = mybir.AluOpType
ACT = mybir.ActivationFunctionType
AX = mybir.AxisListType
F32 = mybir.dt.float32
BF16 = mybir.dt.bfloat16
I32 = mybir.dt.int32

N = 3125
E = 50000
D = 256
HID = 512
EF = 16
NW = -(-N // P)
NPAD = NW * P
TAIL = N - (NW - 1) * P
EPS = 1e-5

CH = 7
COLS = 392
FULLP = E // COLS
LASTC = E - FULLP * COLS
PADKEY = NW * P
BINS = NW + 1
NT = -(-E // P) + NW
LT = NT + 2
HALVES = COLS // (2 * CH)
SPLITS = 6
ROW = 2 + SPLITS * EF // 2
EW = SPLITS * EF

U = 8
LC = 4
assert COLS * P >= E + 0 and COLS * P - E <= 2 * P and HALVES * 2 * CH == COLS and NT % U == 0


def blocks(eng, count, unroll, lo, hi, body):
    for i in range(lo):
        for j in range(unroll):
            body(i, j)
    with eng.Fori(lo, hi) as i:
        for j in range(unroll):
            body(i, j)
    for i in range(hi, -(-count // unroll)):
        for j in range(unroll):
            if i * unroll + j < count:
                body(i, j)


def inside(i, j, unroll, n):
    return not isinstance(i, int) or 0 <= i * unroll + j < n


def hold(pool, turn):
    pool.sem_inc(turn, 1)


class Names:

    def __init__(self, nc, stack):
        self.nc, self.stack = nc, stack

    def sb(self, name, shape, dt=F32):
        return self.stack.enter_context(self.nc.sbuf_tensor(name, shape, dt))

    def ps(self, name, shape, dt=F32):
        return self.stack.enter_context(self.nc.psum_tensor(name, shape, dt))

    def sem(self, name):
        return self.stack.enter_context(self.nc.semaphore(name))


class Chain:

    def __init__(self, eng, sem):
        self.eng, self.sem, self.n = eng, sem, 0

    def __call__(self, ins):
        self.n += 1
        ins.then_inc(self.sem, 1)
        self.eng.wait_ge(self.sem, self.n)


def sort_and_embed(nc, io, dr, keep):
    with ExitStack() as stack:
        g = Names(nc, stack)
        key = [g.sb(f"key{n}", [P, COLS], I32) for n in range(2)]
        key_hi = g.sb("key_hi", [P, COLS], I32)
        key_lo_w = g.sb("key_lo", [P, LT], I32)
        key_lo = key_lo_w[:, 0:COLS]
        hi16 = g.sb("hi16", [P, COLS], BF16)
        lo16 = [g.sb(f"lo16_{n}", [P, COLS], BF16) for n in range(2)]
        onehot_hi = [g.sb(f"onehot_hi{n}", [P, BINS, COLS], BF16) for n in range(2)]
        count = keep.A[:, :, :].rearrange("p s n -> p (s n)")[:, 0:2 * BINS * COLS].bitcast(F32)
        count3 = count.rearrange("p (b t) -> p b t", b=BINS)
        posf_w = g.sb("posf", [P, LT])
        posf = posf_w[:, 0:COLS]
        posi, pos_lo = key_hi, key_lo
        row_src = g.sb("row_src", [P, COLS], I32)
        tot = g.sb("tot", [P, BINS])
        before = g.sb("before", [P, BINS])
        tiles_i = g.sb("tiles_i", [P, NW], I32)
        tiles_f = g.sb("tiles_f", [P, NW])
        tiles_end = g.sb("tiles_end", [P, NW])
        start = g.sb("start", [P, BINS])
        offset = g.sb("offset", [P, BINS])
        tile_no = key_lo_w[0:1, 0:NT]
        tile_nof = g.sb("tile_nof", [1, NT])
        tile_win = posf_w[0:1, 0:NT]
        feat = g.sb("feat", [P, 2, 2 * CH, EF])
        ring = g.sb("ring", [P, 2, CH, ROW])
        ring16 = ring[:, :, :, :].rearrange("p s t w -> p (s t w)").bitcast(BF16).rearrange(
            "p (s t w) -> p s t w", s=2, t=CH)
        ring_i = ring[:, :, :, :].rearrange("p s t w -> p (s t w)").bitcast(I32).rearrange(
            "p (s t w) -> p s t w", s=2, t=CH)
        ring_row = g.sb("ring_row", [P, 2, CH], I32)
        rest = g.sb("rest", [P, 2, CH, EF])
        FR = 11
        fill = g.sb("fill", [P, FR, ROW])
        fill_d = keep.pair_w
        assert LT % FR == 0
        iota_i = g.sb("iota_i", [P, P], I32)
        part_i = g.sb("part_i", [P, 1], I32)
        part = g.sb("part", [P, 1])
        before_m = g.sb("before_m", [P, P])
        ones = g.sb("ones", [P, P])
        onehot_lo = g.sb("onehot_lo", [P, 4, CH, P], BF16)
        stats = g.sb("stats", [P, NW, 6])
        mv = g.sb("mv", [P, NW, 2])
        std = g.sb("std", [P, NW])
        rstd = g.sb("rstd", [P, NW])
        nmr = g.sb("nmr", [P, NW])
        h = g.sb("h", [P, 2, D])
        hT = g.sb("hT", [P, 2, D])
        w1 = g.sb("w1", [P, 4, HID])
        b1 = g.sb("b1", [P, HID])
        vA = g.sb("vA", [P, HID])
        rA = g.sb("rA", [P, HID])
        bst = g.sb("bst", [P, 2, HID])
        we, we_r = vA[0:EF, :], rA[0:EF, :]
        we_part = [bst[0:EF, :, :].rearrange("p s n -> p (s n)").bitcast(BF16)[:, n * HID:(n + 1) * HID]
                   for n in range(3)]
        pA = [g.ps(f"pA{n}", [P, HID]) for n in range(2)]
        pB = [g.ps(f"pB{n}", [P, HID]) for n in range(2)]
        pT = [g.ps(f"pT{n}", [P, HID]) for n in range(2)]
        pH = [g.ps(f"pH{n}", [P, HID]) for n in range(2)]
        pS = [pT[0], pT[1]]

        keys_set = g.sem("keys_set")
        keys_in = g.sem("keys_in")
        x_in = g.sem("x_in")
        feat_whole = g.sem("feat_whole")
        feat_in = [g.sem(f"feat_in{n}") for n in range(2)]
        w_in = g.sem("w_in")
        x_zero = g.sem("x_zero")
        iota_ready = g.sem("iota_ready")
        fill_ready = g.sem("fill_ready")
        fill_part = g.sem("fill_part")
        filled = g.sem("filled")
        own = g.sem("dve_own")
        consts = g.sem("consts")
        tot_ready = g.sem("tot_ready")
        sums_done = g.sem("sums_done")
        var_ready = g.sem("var_ready")
        std_ready = g.sem("std_ready")
        ln_ready = g.sem("ln_ready")
        payload = g.sem("payload")
        scattered = [g.sem(f"scattered{n}") for n in range(2)]
        oh_ready = g.sem("oh_ready")
        hist_done = g.sem("hist_done")
        h_ready = g.sem("h_ready")
        resid_done = g.sem("resid_done")
        trh_done = g.sem("trh_done")
        ht_ready = g.sem("ht_ready")
        ht_out = [g.sem(f"ht_out{n}") for n in range(2)]
        ab_done = g.sem("ab_done")
        va_ready = g.sem("va_ready")
        a_hi = g.sem("a_hi")
        ra_ready = g.sem("ra_ready")
        a_mid = g.sem("a_mid")
        a_lo = g.sem("a_lo")
        b_ready = g.sem("b_ready")
        b_out = [g.sem(f"b_out{n}") for n in range(2)]
        deg_ready = g.sem("deg_ready")
        sq_ready = g.sem("sq_ready")
        we_parts = g.sem("we_parts")
        we_out = g.sem("we_out")

        def walk(eng, body):
            blocks(eng, HALVES, 2, 1, NW // 2, body)

        block = stack.enter_context(nc.Block())

        @block.sync
        def _(sp):
            sp.wait_ge(keys_set, 2)
            for n, a in enumerate((io["src"], io["dst"])):
                sp.dma_start(key[n][0:FULLP, :], a[0:FULLP * COLS].rearrange("(p t) -> p t", t=COLS)
                             ).then_inc(keys_in, 16)
                sp.dma_start(key[n][FULLP:FULLP + 1, 0:LASTC],
                             a[FULLP * COLS:E].rearrange("(p t) -> p t", p=1)).then_inc(keys_in, 16)
            sp.wait_ge(x_zero, 1)
            sp.dma_start(keep.resid[:, 0:NW - 1, :], io["x"][0:(NW - 1) * P, :].rearrange("(w p) d -> p w d", p=P)
                         ).then_inc(x_in, 16)
            sp.dma_start(keep.resid[0:TAIL, NW - 1, :], io["x"][(NW - 1) * P:N, :]).then_inc(x_in, 16)
            sp.dma_start(w1[:, :, :], io["L0_gnn_mW1"][0:2 * D, :].rearrange("(k p) n -> p k n", p=P)
                         ).then_inc(w_in, 16)
            sp.dma_start(we[:, :], io["L0_gnn_mW1"][2 * D:2 * D + EF, :]).then_inc(w_in, 16)
            sp.dma_start(b1[:, :], io["L0_gnn_mb1"].partition_broadcast(P)).then_inc(w_in, 16)
            sp.wait_ge(fill_ready, 4)
            for n in range(LT // FR):
                sp.dma_start(dr.src_list[:, n * FR:(n + 1) * FR, :], fill[:, :, :]).then_inc(filled, 16)
            sp.dma_start(dr.dst_list[:, :, :], fill_d[:, :, :]).then_inc(filled, 16)

            feat_rows = dr.feat.rearrange("(p t) f -> p (t f)", t=COLS)

            def load_feat(i, j):
                s = 2 * i + j
                if not isinstance(i, int) or s >= 2:
                    sp.wait_ge(payload, 14 * (s - 1))
                sp.dma_start(feat[:, j, :, :].rearrange("p t f -> p (t f)"),
                             feat_rows[:, bass.ds(s * 2 * CH * EF, 2 * CH * EF)]).then_inc(feat_in[j], 16)

            def step(i, j):
                load_feat(i, j)
                if inside(i, j - 1, 2, NW):
                    sp.wait_ge(ht_ready, 2 * i + j)
                    sp.dma_start(dr.hT[bass.ds(2 * i + j - 1, 1), :, :].rearrange("w p n -> p (w n)"),
                                 hT[:, (j - 1) % 2, :]).then_inc(ht_out[(j - 1) % 2], 16)
                if inside(i, j - 2, 2, NW):
                    sp.wait_ge(b_ready, 2 * i + j - 1)
                    sp.dma_start(dr.B[bass.ds((2 * i + j - 2) * P, P), :], bst[:, j % 2, :]
                                 ).then_inc(b_out[j % 2], 16)

            sp.wait_ge(feat_whole, 48)
            sp.wait_ge(we_parts, 1)
            for s, which in enumerate((0, 1, 2, 0, 1, 0)):
                sp.dma_start(keep.we[s * EF:(s + 1) * EF, :], we_part[which][:, :]).then_inc(we_out, 16)
            walk(sp, step)
            sp.wait_ge(we_out, 16 * SPLITS)
            for q in ht_out:
                sp.wait_ge(q, 16 * (NW // 2))
            sp.wait_ge(ht_out[0], 16 * (NW - NW // 2))
            sp.wait_ge(b_out[0], 16 * (NW - NW // 2))
            sp.wait_ge(b_out[1], 16 * (NW // 2))

        @block.gpsimd
        def _(pool):
            turn = g.sem("turn_sort")
            for n in range(2):
                nc.gpsimd.memset(key[n][:, :], PADKEY).then_inc(keys_set, 1)
            nc.gpsimd.memset(keep.resid[:, NW - 1, :], 0.0).then_inc(x_zero, 1)
            nc.gpsimd.iota(iota_i[:, :], [[1, P]], base=0, channel_multiplier=0).then_inc(iota_ready, 1)
            nc.gpsimd.iota(part_i[:, :], [[0, 1]], base=0, channel_multiplier=1).then_inc(iota_ready, 1)
            nc.gpsimd.iota(tile_no[:, :], [[1, NT]], base=0, channel_multiplier=0).then_inc(iota_ready, 1)
            nc.gpsimd.memset(fill[:, :, :], 0.0).then_inc(fill_part, 1)
            nc.gpsimd.memset(fill_d[:, :, :], 0.0).then_inc(fill_part, 1)
            pool.wait_ge(fill_part, 2)
            pool.wait_ge(feat_whole, 48)
            nc.gpsimd.memset(fill[:, :, 0:1], -1.0).then_inc(fill_ready, 2)
            nc.gpsimd.memset(fill_d[:, :, 1:2], -1.0).then_inc(fill_ready, 2)
            pool.wait_ge(filled, 16 * (LT // FR + 1))
            with pool.Fori(0, HALVES) as i:
                for c in range(2):
                    pool.wait_ge(payload, i * 14 + 7 * c + 7)
                    hold(pool, turn)
                    for t in range(CH):
                        nc.gpsimd.indirect_dma_start(
                            dr.src_list[:, :, :].rearrange("p t w -> (p t) w"),
                            bass.IndirectOffsetOnAxis(ap=ring_row[:, c, t:t + 1], axis=0),
                            ring[:, c, t, :], None).then_inc(scattered[c], 16)
            for q in scattered:
                pool.wait_ge(q, 16 * CH * HALVES)

        @block.scalar
        def _(act):
            act.dma_start(dr.feat[0:E, :].rearrange("(p t) f -> p (t f)", t=E // 16),
                          io["edge_attr_16"].rearrange("(p t) f -> p (t f)", t=E // 16)).then_inc(feat_whole, 16)
            act.wait_ge(fill_part, 2)
            act.dma_start(dr.feat[E:E + P, :], fill[:, 0, 0:EF]).then_inc(feat_whole, 16)
            act.dma_start(dr.feat[E + P:COLS * P, :], fill[0:COLS * P - E - P, 0, 0:EF]).then_inc(feat_whole, 16)
            act.wait_ge(var_ready, 1)
            nc.scalar.activation(std[:, :], std[:, :], ACT.Sqrt).then_inc(std_ready, 1)
            act.wait_ge(ln_ready, 2)

            def step(i, j):
                s = 2 * i + j
                if inside(i, j, 2, NW):
                    if not isinstance(i, int) or s >= 2:
                        act.wait_ge(trh_done, s - 1)
                        act.wait_ge(resid_done, s - 1)
                    nc.scalar.activation(h[:, j, :], keep.resid[:, bass.ds(s, 1), :].rearrange("p w d -> p (w d)"),
                                         ACT.Relu, bias=nmr[:, bass.ds(s, 1)], scale=rstd[:, bass.ds(s, 1)]
                                         ).then_inc(h_ready, 1)
                if inside(i, j - 1, 2, NW):
                    b = (j - 1) % 2
                    act.wait_ge(trh_done, s)
                    if not isinstance(i, int) or s >= 3:
                        act.wait_ge(ab_done, s - 2)
                        act.wait_ge(ht_out[b], 16 * (i + (j - 1) // 2))
                    nc.scalar.copy(hT[:, b, :], pT[b][:, 0:D]).then_inc(ht_ready, 1)
                if inside(i, j - 2, 2, NW):
                    act.wait_ge(va_ready, s - 1)
                    nc.scalar.copy(keep.A[:, 0, bass.ds((s - 2) * HID, HID)], vA[:, :]).then_inc(a_hi, 1)
                    act.wait_ge(ab_done, s - 1)
                    if not isinstance(i, int) or s >= 4:
                        act.wait_ge(b_out[j], 16 * (i - 1))
                    if isinstance(i, int) and s == 2:
                        act.wait_ge(we_out, 16 * SPLITS)
                    nc.scalar.copy(bst[:, j, :], pB[j][:, :]).then_inc(b_ready, 1)
                    act.wait_ge(ra_ready, s - 1)
                    nc.scalar.copy(keep.A[:, 1, bass.ds((s - 2) * HID, HID)], rA[:, :]).then_inc(a_mid, 1)

            walk(act, step)
            act.wait_ge(deg_ready, 2)
            nc.scalar.activation(keep.dis[:, :], keep.dis[:, :], ACT.Sqrt).then_inc(sq_ready, 1)

        @block.vector
        def _(dve):
            v = nc.vector
            link = Chain(dve, own)
            dve.wait_ge(iota_ready, 3)
            link(v.tensor_copy(keep.iota[:, :], iota_i[:, :]))
            link(v.tensor_copy(part[:, :], part_i[:, :]))
            v.tensor_copy(keep.iota16[:, :], keep.iota[:, :]).then_inc(consts, 1)
            v.tensor_scalar(keep.ident[:, :], keep.iota[:, :], part[:, 0:1], None, ALU.is_equal).then_inc(consts, 1)
            v.tensor_scalar(keep.ident16[:, :], keep.iota[:, :], part[:, 0:1], None, ALU.is_equal).then_inc(consts, 1)
            v.tensor_scalar(before_m[:, :], keep.iota[:, :], part[:, 0:1], None, ALU.is_gt).then_inc(consts, 1)
            v.memset(ones[:, :], 1.0).then_inc(consts, 1)
            v.tensor_copy(tile_nof[:, :], tile_no[:, :]).then_inc(consts, 1)
            dve.wait_ge(consts, 6)

            def positions(n, row, tile_map):
                link(v.tensor_scalar(key_hi[:, :], key[n][:, :], 7, None, ALU.arith_shift_right))
                link(v.tensor_scalar(key_lo[:, :], key[n][:, :], P - 1, None, ALU.bitwise_and))
                link(v.tensor_copy(hi16[:, :], key_hi[:, :]))
                link(v.tensor_copy(lo16[n][:, :], key_lo[:, :]))
                for b in range(BINS):
                    last = v.tensor_scalar(onehot_hi[n][:, b, :], hi16[:, :], float(b), None, ALU.is_equal)
                    if b < BINS - 1:
                        last.then_inc(own, 1)
                        link.n += 1
                link(last)
                flat = onehot_hi[n][:, :, :].rearrange("p b t -> p (b t)")
                link(v.tensor_tensor_scan(count, flat, flat, 0.0, ALU.add, ALU.max))
                ends = count3[:, :, COLS - 1]
                link(v.tensor_copy(tot[:, :], ends))
                link(v.tensor_tensor(tot[:, 1:BINS], tot[:, 1:BINS], count3[:, 0:BINS - 1, COLS - 1], ALU.subtract))
                v.tensor_copy(tot[:, 0:1], tot[:, 0:1]).then_inc(tot_ready, 1)
                dve.wait_ge(sums_done, n + 1)
                link(v.tensor_scalar(tiles_i[:, :], pS[1][:, 0:NW], float(P - 1), None, ALU.add))
                link(v.tensor_scalar(tiles_i[:, :], tiles_i[:, :], 7, None, ALU.arith_shift_right))
                link(v.tensor_copy(tiles_f[:, :], tiles_i[:, :]))
                link(v.tensor_tensor_scan(tiles_end[:, :], tiles_f[:, :], tiles_f[:, :], 0.0, ALU.add, ALU.max))
                link(v.memset(start[:, NW:BINS], float(NT)))
                link(v.tensor_tensor(start[:, 0:NW], tiles_end[:, :], tiles_f[:, :], ALU.subtract))
                link(v.scalar_tensor_tensor(out=offset[:, :], in0=start[:, :], scalar=float(P),
                                            in1=pS[0][:, 0:BINS], op0=ALU.mult, op1=ALU.add))
                link(v.tensor_scalar(offset[:, :], offset[:, :], -1.0, None, ALU.add))
                link(v.tensor_tensor(offset[:, 1:BINS], offset[:, 1:BINS], count3[:, 0:BINS - 1, COLS - 1],
                                     ALU.subtract))
                for b in range(BINS):
                    last = v.scalar_tensor_tensor(out=count3[:, b, :], in0=count3[:, b, :], scalar=offset[:, b:b + 1],
                                                  in1=onehot_hi[n][:, b, :], op0=ALU.add, op1=ALU.mult)
                    if b < BINS - 1:
                        last.then_inc(own, 1)
                        link.n += 1
                link(last)
                link(v.tensor_reduce(posf[:, :], count3.rearrange("p b t -> p t b"), AX.X, ALU.add))
                link(v.tensor_copy(posi[:, :], posf[:, :]))
                link(v.tensor_scalar(pos_lo[:, :], posi[:, :], P - 1, None, ALU.bitwise_and))
                link(v.tensor_scalar(posi[:, :], posi[:, :], 7, None, ALU.arith_shift_right))
                link(v.scalar_tensor_tensor(out=row[:, :], in0=pos_lo[:, :], scalar=float(LT), in1=posi[:, :],
                                            op0=ALU.mult, op1=ALU.add))
                link(v.memset(tile_win[:, :], 0.0))
                for b in range(NW - 1):
                    link(v.scalar_tensor_tensor(out=tile_win[:, :], in0=tile_nof[:, :], scalar=tiles_end[0:1, b:b + 1],
                                                in1=tile_win[:, :], op0=ALU.is_ge, op1=ALU.add))
                link(v.tensor_copy(tile_map[:, :], tile_win[:, :]))

            dve.wait_ge(keys_in, 64)
            positions(0, row_src, keep.src_map)

            dve.wait_ge(x_in, 32)
            for w in range(NW):
                link(v.bn_stats(stats[:, w, :], keep.resid[:, w, :]))
            for w in range(NW):
                link(v.bn_aggr(mv[:, w, :], stats[:, w, :]))
            v.tensor_scalar(std[:, :], mv[:, :, 1], EPS, None, ALU.add).then_inc(var_ready, 1)
            dve.wait_ge(std_ready, 1)
            v.reciprocal(rstd[:, :], std[:, :]).then_inc(ln_ready, 1)
            dve.wait_ge(ln_ready, 1)
            v.scalar_tensor_tensor(out=nmr[:, :], in0=mv[:, :, 0], scalar=-1.0, in1=rstd[:, :],
                                   op0=ALU.mult, op1=ALU.mult).then_inc(ln_ready, 1)

            dve.wait_ge(w_in, 48)
            link(v.tensor_copy(we_part[0][:, :], we[:, :]))
            link(v.tensor_tensor(we_r[:, :], we[:, :], we_part[0][:, :], ALU.subtract))
            link(v.tensor_copy(we_part[1][:, :], we_r[:, :]))
            v.tensor_tensor(we_part[2][:, :], we_r[:, :], we_part[1][:, :], ALU.subtract).then_inc(we_parts, 1)

            positions(1, keep.row_dst, keep.dst_map)
            dve.wait_ge(filled, 16 * (LT // FR + 1))
            link(v.tensor_copy(keep.pair_i[:, :, 0], key[0][:, :]))
            link(v.tensor_copy(keep.pair[:, :, 1], lo16[1][:, :]))

            def step(i, j):
                s = 2 * i + j
                dve.wait_ge(feat_in[j], 16 * (i + 1))
                for c in range(2):
                    if not isinstance(i, int) or s > 0:
                        dve.wait_ge(scattered[c], (16 * CH) * s)
                    done = s * 14 + 7 * c
                    t0 = (2 * s + c) * CH
                    e = feat[:, j, c * CH:(c + 1) * CH, :]
                    f16 = ring16[:, c, :, :]
                    hi3 = f16[:, :, 4:4 + 3 * EF].rearrange("p t (r f) -> p t r f", r=3)
                    mid2 = f16[:, :, 4 + 3 * EF:4 + 5 * EF].rearrange("p t (r f) -> p t r f", r=2)
                    v.tensor_copy(hi3, e.unsqueeze(2).to_broadcast([P, CH, 3, EF])).then_inc(payload, 1)
                    v.tensor_copy(ring[:, c, :, 0], lo16[0][:, bass.ds(t0, CH)]).then_inc(payload, 1)
                    v.tensor_copy(ring_i[:, c, :, 1], key[1][:, bass.ds(t0, CH)]).then_inc(payload, 1)
                    v.tensor_copy(ring_row[:, c, :], row_src[:, bass.ds(t0, CH)]).then_inc(payload, 1)
                    dve.wait_ge(payload, done + 4)
                    v.tensor_tensor(rest[:, c, :, :], e, f16[:, :, 4:4 + EF], ALU.subtract).then_inc(payload, 1)
                    dve.wait_ge(payload, done + 5)
                    v.tensor_copy(mid2, rest[:, c, :, :].unsqueeze(2).to_broadcast([P, CH, 2, EF])
                                  ).then_inc(payload, 1)
                    dve.wait_ge(payload, done + 6)
                    v.tensor_tensor(f16[:, :, 4 + 5 * EF:4 + 6 * EF], rest[:, c, :, :],
                                    f16[:, :, 4 + 3 * EF:4 + 4 * EF], ALU.subtract).then_inc(payload, 1)
                for c in range(2):
                    for n in range(2):
                        k = 2 * c + n
                        if not isinstance(i, int) or s > 0:
                            dve.wait_ge(hist_done, 4 * s + k - 3)
                        lo = lo16[n][:, bass.ds((2 * s + c) * CH, CH)]
                        v.tensor_tensor(onehot_lo[:, k, :, :], lo.unsqueeze(2).to_broadcast([P, CH, P]),
                                        keep.iota16[:, :].unsqueeze(1).to_broadcast([P, CH, P]), ALU.is_equal
                                        ).then_inc(oh_ready, 1)
                if inside(i, j - 1, 2, NW):
                    dve.wait_ge(h_ready, s)
                    r = keep.resid[:, bass.ds(s - 1, 1), :].rearrange("p w d -> p (w d)")
                    v.tensor_tensor(r, r, h[:, (j - 1) % 2, :], ALU.add).then_inc(resid_done, 1)
                if inside(i, j - 2, 2, NW):
                    dve.wait_ge(ab_done, s - 1)
                    v.tensor_tensor(vA[:, :], pA[j][:, :], b1[:, :], ALU.add).then_inc(va_ready, 1)
                    dve.wait_ge(a_hi, s - 1)
                    if not isinstance(i, int) or s > 2:
                        dve.wait_ge(a_mid, s - 2)
                    v.tensor_tensor(rA[:, :], vA[:, :], keep.A[:, 0, bass.ds((s - 2) * HID, HID)], ALU.subtract
                                    ).then_inc(ra_ready, 1)
                    dve.wait_ge(a_mid, s - 1)
                    v.tensor_tensor(keep.A[:, 2, bass.ds((s - 2) * HID, HID)], rA[:, :],
                                    keep.A[:, 1, bass.ds((s - 2) * HID, HID)], ALU.subtract).then_inc(a_lo, 1)

            walk(dve, step)
            dve.wait_ge(hist_done, 4 * HALVES)
            v.tensor_copy(keep.deg_src[:, :], pH[0][:, 0:NW]).then_inc(deg_ready, 1)
            v.tensor_scalar(keep.dis[:, :], pH[1][:, 0:NW], 1.0, None, ALU.add).then_inc(deg_ready, 1)
            dve.wait_ge(sq_ready, 1)
            link(v.reciprocal(keep.dis[:, :], keep.dis[:, :]))

        @block.tensor
        def _(pe):
            mm = nc.tensor.matmul
            pe.wait_ge(consts, 6)
            for n in range(2):
                pe.wait_ge(tot_ready, n + 1)
                mm(pS[0][:, 0:BINS], before_m[:, :], tot[:, :], start=True, stop=True)
                mm(pS[1][:, 0:BINS], ones[:, :], tot[:, :], start=True, stop=True).then_inc(sums_done, 1)

            pe.wait_ge(payload, 1)

            def step(i, j):
                s = 2 * i + j
                if inside(i, j, 2, NW):
                    pe.wait_ge(h_ready, s + 1)
                    if not isinstance(i, int) or s >= 2:
                        pe.wait_ge(ht_ready, s - 1)
                    for k in range(2):
                        last = nc.tensor.transpose(pT[j][:, k * P:(k + 1) * P], h[:, j, k * P:(k + 1) * P],
                                                   keep.ident[:, :])
                    last.then_inc(trh_done, 1)
                if inside(i, j - 1, 2, NW):
                    b = (j - 1) % 2
                    pe.wait_ge(ht_ready, s)
                    if not isinstance(i, int) or s >= 3:
                        pe.wait_ge(va_ready, s - 2)
                        pe.wait_ge(b_ready, s - 2)
                    if isinstance(i, int) and s == 1:
                        pe.wait_ge(w_in, 48)
                    for out, k0 in ((pA[b], 0), (pB[b], 2)):
                        for k in range(2):
                            last = mm(out[:, :], hT[:, b, k * P:(k + 1) * P], w1[:, k0 + k, :],
                                      start=(k == 0), stop=(k == 1))
                    last.then_inc(ab_done, 1)
                for c in range(2):
                    for n in range(2):
                        pe.wait_ge(oh_ready, 4 * s + 2 * c + n + 1)
                        for t in range(CH):
                            first = isinstance(i, int) and s == 0 and c == 0 and t == 0
                            end = isinstance(i, int) and s == HALVES - 1 and c == 1 and t == CH - 1
                            rhs = onehot_hi[n][:, 0:NW, bass.ds((2 * s + c) * CH + t, 1)].rearrange("p b t -> p (b t)")
                            last = mm(pH[n][:, 0:NW], onehot_lo[:, 2 * c + n, t, :], rhs, start=first, stop=end,
                                      skip_group_check=True)
                        last.then_inc(hist_done, 1)

            walk(pe, step)


def edge_mlp(nc, io, dr, keep):
    with ExitStack() as stack:
        g = Names(nc, stack)
        S = keep.S
        rows = g.sb("rows", [P, 2, LC, ROW])
        rows_i = rows[:, :, :, :].rearrange("p s t w -> p (s t w)").bitcast(I32).rearrange(
            "p (s t w) -> p s t w", s=2, t=LC)
        rows16 = rows[:, :, :, :].rearrange("p s t w -> p (s t w)").bitcast(BF16).rearrange(
            "p (s t w) -> p s t w", s=2, t=LC)
        brow = g.sb("brow", [P, 4, HID])
        oh16 = g.sb("oh16", [P, 4, P], BF16)
        oh32 = g.sb("oh32", [P, 4, P])
        turned = g.sb("turned", [P, 2, 2 * P], BF16)
        pre = g.sb("pre", [P, 2, HID])
        hid = g.sb("hid", [P, 2, HID])
        d_pair = g.sb("d_pair", [P, 2, LC, 2])
        d_row = g.sb("d_row", [P, 2, LC], I32)
        pT = [g.ps(f"pTurn{n}", [P, 2 * HID], BF16) for n in range(2)]
        pE = [g.ps(f"pEdge{n}", [P, HID]) for n in range(2)]
        pN = [g.ps(f"pNode{n}", [P, HID]) for n in range(2)]

        s_zero = g.sem("s_zero")
        rows_in = [g.sem(f"rows_in{n}") for n in range(2)]
        b_in = [g.sem(f"b_in{n}") for n in range(4)]
        oh_ready = g.sem("oh_ready2")
        turn_done = g.sem("turn_done")
        turn_copied = g.sem("turn_copied")
        edge_done = g.sem("edge_done")
        pre_ready = g.sem("pre_ready")
        hid_ready = g.sem("hid_ready")
        node_done = g.sem("node_done")
        s_added = g.sem("s_added")
        d_copied = g.sem("d_copied")
        d_out = [g.sem(f"d_out{n}") for n in range(2)]
        LAST = NT // U - 1

        block = stack.enter_context(nc.Block())

        @block.sync
        def _(sp):
            def step(i, j):
                if j % LC:
                    return
                b = j // LC
                if not isinstance(i, int) or i > 0:
                    sp.wait_ge(pre_ready, U * i + j - LC)
                sp.dma_start(rows[:, b, :, :], dr.src_list[:, bass.ds(U * i + j, LC), :]).then_inc(rows_in[b], 16)

            blocks(sp, NT, U, 1, LAST, step)

        @block.gpsimd
        def _(pool):
            turn = g.sem("turn_edge")

            def step(i, j):
                if j % LC == 0:
                    pool.wait_ge(rows_in[j // LC], 16 * (i + 1))
                if not isinstance(i, int) or i > 0 or j >= 4:
                    pool.wait_ge(pre_ready, U * i + j - 3)
                hold(pool, turn)
                nc.gpsimd.indirect_dma_start(
                    brow[:, j % 4, :], None, dr.B,
                    bass.IndirectOffsetOnAxis(ap=rows_i[:, j // LC, j % LC, 1:2], axis=0)).then_inc(b_in[j % 4], 16)

            def pairs_step(i, j):
                c = j // LC
                if j % LC == 0:
                    if not isinstance(i, int) or i > 0:
                        pool.wait_ge(d_out[c], 16 * LC * i)
                    nc.gpsimd.tensor_copy(d_pair[:, c, :, :].rearrange("p t w -> p (t w)"),
                                          keep.pair_flat[:, bass.ds(2 * (U * i + j), 2 * LC)]).then_inc(d_copied, 1)
                    nc.gpsimd.tensor_copy(d_row[:, c, :], keep.row_dst[:, bass.ds(U * i + j, LC)]
                                          ).then_inc(d_copied, 1)
                    pool.wait_ge(d_copied, 4 * i + 2 * c + 2)
                    hold(pool, turn)
                nc.gpsimd.indirect_dma_start(
                    dr.dst_list[:, :, :].rearrange("p t w -> (p t) w"),
                    bass.IndirectOffsetOnAxis(ap=d_row[:, c, j % LC:j % LC + 1], axis=0),
                    d_pair[:, c, j % LC, :], None).then_inc(d_out[c], 16)

            for j in range(U):
                step(0, j)
            with pool.Fori(0, COLS // U) as i:
                for j in range(U):
                    step(i + 1, j)
                    pairs_step(i, j)
            for i in range(COLS // U + 1, NT // U):
                for j in range(U):
                    step(i, j)
            for q in d_out:
                pool.wait_ge(q, 16 * LC * (COLS // U))

        @block.tensor
        def _(pe):
            mm = nc.tensor.matmul

            def step(i, j):
                t = U * i + j
                if inside(i, j, U, NT):
                    pe.wait_ge(oh_ready, 2 * t + 2)
                    if not isinstance(i, int) or t >= 2:
                        pe.wait_ge(turn_copied, t - 1)
                    nc.tensor.transpose(pT[j % 2][:, 0:P], oh16[:, j % 4, :], keep.ident16[:, :])
                    nc.tensor.transpose(pT[j % 2][0:EW, P:2 * P], rows16[:, j // LC, j % LC, 4:4 + EW],
                                        keep.ident16[:, :]).then_inc(turn_done, 1)
                if inside(i, j - 1, U, NT):
                    b = (j - 1) % 2
                    pe.wait_ge(turn_copied, t)
                    if not isinstance(i, int) or t >= 3:
                        pe.wait_ge(pre_ready, t - 2)
                    w = pe.value_load(keep.src_map[0:1, bass.ds(t - 1, 1)], min_val=0, max_val=NW - 1)
                    mm(pE[b][:, :], turned[0:EW, b, P:2 * P], keep.we[:, :], start=True, stop=False)
                    for k in range(3):
                        last = mm(pE[b][:, :], turned[:, b, 0:P], keep.A[:, k, bass.ds(w * HID, HID)],
                                  start=False, stop=(k == 2))
                    last.then_inc(edge_done, 1)
                if inside(i, j - 2, U, NT):
                    pe.wait_ge(hid_ready, t - 1)
                    if not isinstance(i, int) or t >= 4:
                        pe.wait_ge(s_added, t - 3)
                    mm(pN[j % 2][:, :], oh32[:, (j - 2) % 4, :], hid[:, j % 2, :], start=True, stop=True
                       ).then_inc(node_done, 1)

            blocks(pe, NT + 2, U, 1, LAST, step)

        @block.scalar
        def _(act):
            def step(i, j):
                t = U * i + j
                if inside(i, j, U, NT):
                    act.wait_ge(turn_done, t + 1)
                    if not isinstance(i, int) or t >= 2:
                        act.wait_ge(edge_done, t - 1)
                    nc.scalar.copy(turned[:, j % 2, 0:P], pT[j % 2][:, 0:P])
                    nc.scalar.copy(turned[0:EW, j % 2, P:2 * P], pT[j % 2][0:EW, P:2 * P]).then_inc(turn_copied, 1)
                if inside(i, j - 1, U, NT):
                    b = (j - 1) % 2
                    act.wait_ge(pre_ready, t)
                    if not isinstance(i, int) or t >= 3:
                        act.wait_ge(node_done, t - 2)
                    nc.scalar.activation(hid[:, b, :], pre[:, b, :], ACT.Relu).then_inc(hid_ready, 1)

            blocks(act, NT + 1, U, 1, LAST, step)

        @block.vector
        def _(dve):
            v = nc.vector
            v.memset(S[:, :], 0.0).then_inc(s_zero, 1)
            dve.wait_ge(s_zero, 1)

            def step(i, j):
                t = U * i + j
                if inside(i, j - 4, U, NT):
                    dve.wait_ge(node_done, t - 3)
                    if not isinstance(i, int) or t > 4:
                        dve.wait_ge(s_added, t - 4)
                    w = dve.value_load(keep.src_map[0:1, bass.ds(t - 4, 1)], min_val=0, max_val=NW - 1)
                    sw = S[:, bass.ds(w * HID, HID)]
                    v.tensor_tensor(sw, sw, pN[j % 2][:, :], ALU.add).then_inc(s_added, 1)
                if inside(i, j, U, NT):
                    if j % LC == 0:
                        dve.wait_ge(rows_in[j // LC], 16 * (i + 1))
                    lo = rows[:, j // LC, j % LC, 0:1]
                    v.tensor_scalar(oh16[:, j % 4, :], keep.iota16[:, :], lo, None, ALU.is_equal).then_inc(oh_ready, 1)
                    v.tensor_scalar(oh32[:, j % 4, :], keep.iota[:, :], lo, None, ALU.is_equal).then_inc(oh_ready, 1)
                if inside(i, j - 2, U, NT):
                    b = (j - 2) % 2
                    dve.wait_ge(edge_done, t - 1)
                    dve.wait_ge(b_in[(j - 2) % 4], 16 * (i * (U // 4) + (j - 2) // 4 + 1))
                    if not isinstance(i, int) or t >= 4:
                        dve.wait_ge(hid_ready, t - 3)
                    v.tensor_tensor(pre[:, b, :], pE[b][:, :], brow[:, (j - 2) % 4, :], ALU.add
                                    ).then_inc(pre_ready, 1)

            blocks(dve, NT + 4, U, 1, LAST, step)
            dve.wait_ge(s_added, NT)


def node_mlp(nc, io, dr, keep):
    with ExitStack() as stack:
        g = Names(nc, stack)
        mw2 = g.sb("mw2", [P, 4, D])
        uw1 = g.sb("uw1", [P, 4, HID])
        uw2 = g.sb("uw2", [P, 4, D])
        mb2 = g.sb("mb2", [P, D])
        ub2 = g.sb("ub2", [P, D])
        ub1 = g.sb("ub1", [P, 4])
        hT = g.sb("hT3", [P, 2, D])
        s_win = g.sb("s_win", [P, 2, HID])
        sT = g.sb("sT", [P, 2, HID])
        agg = g.sb("agg", [P, 2, D])
        aggT = g.sb("aggT", [P, 2, D])
        uT = g.sb("uT", [P, 2, HID])
        xm = g.sb("xm", [P, D])
        stats = g.sb("stats3", [P, NW, 6])
        mv = g.sb("mv3", [P, NW, 2])
        std = g.sb("std3", [P, NW])
        pS = [g.ps(f"pS3_{n}", [P, HID]) for n in range(2)]
        pU = [g.ps(f"pU3_{n}", [P, HID]) for n in range(2)]
        pX = [g.ps(f"pX3_{n}", [P, HID]) for n in range(2)]
        pG = g.ps("pG3", [P, HID])
        pR = g.ps("pR3", [P, HID])

        w_in = g.sem("w_in3")
        h_in = [g.sem(f"h_in3_{n}") for n in range(2)]
        s_copied = g.sem("s_copied")
        st_done = g.sem("st_done")
        st_ready = g.sem("st_ready")
        agg_done = g.sem("agg_done")
        agg_ready = g.sem("agg_ready")
        at_done = g.sem("at_done")
        at_ready = g.sem("at_ready")
        u_done = g.sem("u_done")
        u_ready = g.sem("u_ready")
        x_done = g.sem("x_done")
        xm_ready = g.sem("xm_ready")
        x_ready = g.sem("x_ready")
        stat_ready = g.sem("stat_ready")
        own = g.sem("own3")
        var_ready = g.sem("var_ready3")
        std_ready = g.sem("std_ready3")

        def walk(eng, body):
            blocks(eng, NW + 4, 2, 3, NW // 2, body)

        block = stack.enter_context(nc.Block())

        @block.sync
        def _(sp):
            sp.dma_start(mw2[:, :, :], io["L0_gnn_mW2"].rearrange("(k p) n -> p k n", p=P)).then_inc(w_in, 16)
            sp.dma_start(mb2[:, :], io["L0_gnn_mb2"].partition_broadcast(P)).then_inc(w_in, 16)
            sp.dma_start(uw1[:, :, :], io["L0_gnn_uW1"].rearrange("(k p) n -> p k n", p=P)).then_inc(w_in, 16)
            sp.dma_start(uw2[:, :, :], io["L0_gnn_uW2"].rearrange("(k p) n -> p k n", p=P)).then_inc(w_in, 16)
            sp.dma_start(ub2[:, :], io["L0_gnn_ub2"].partition_broadcast(P)).then_inc(w_in, 16)
            for k in range(4):
                sp.dma_start(ub1[:, k:k + 1], io["L0_gnn_ub1"][k * P:(k + 1) * P].rearrange("(p o) -> p o", o=1)
                             ).then_inc(w_in, 16)

            def step(i, j):
                if inside(i, j, 2, NW):
                    s = 2 * i + j
                    if not isinstance(i, int) or s >= 2:
                        sp.wait_ge(u_done, s - 1)
                    sp.dma_start(hT[:, j, :], dr.hT[bass.ds(s, 1), :, :].rearrange("w p n -> p (w n)")
                                 ).then_inc(h_in[j], 16)

            walk(sp, step)

        @block.gpsimd
        def _(pool):
            def step(i, j):
                if inside(i, j, 2, NW):
                    s = 2 * i + j
                    if not isinstance(i, int) or s >= 2:
                        pool.wait_ge(st_done, s - 1)
                    nc.gpsimd.tensor_copy(s_win[:, j, :], keep.S[:, bass.ds(s * HID, HID)]).then_inc(s_copied, 1)

            walk(pool, step)

        @block.tensor
        def _(pe):
            mm = nc.tensor.matmul
            pe.wait_ge(w_in, 16 * 9)

            def step(i, j):
                s = 2 * i + j
                looped = not isinstance(i, int)
                if inside(i, j - 4, 2, NW):
                    pe.wait_ge(u_ready, 4 * (s - 3))
                    if looped or s >= 6:
                        pe.wait_ge(xm_ready, s - 5)
                    for k in range(4):
                        last = mm(pX[j][:, 0:D], uT[:, j, k * P:(k + 1) * P], uw2[:, k, :], start=(k == 0), stop=(k == 3))
                    last.then_inc(x_done, 1)
                if inside(i, j - 3, 2, NW):
                    b = (j - 3) % 2
                    pe.wait_ge(at_ready, s - 2)
                    pe.wait_ge(h_in[b], 16 * (i + (j - 3) // 2 + 1))
                    if looped or s >= 5:
                        pe.wait_ge(u_ready, 4 * (s - 4))
                    for m in range(4):
                        for k in range(4):
                            rhs = (hT if k < 2 else aggT)[:, b, (k % 2) * P:(k % 2 + 1) * P]
                            last = mm(pU[b][:, m * P:(m + 1) * P], uw1[:, k, m * P:(m + 1) * P], rhs,
                                      start=(k == 0), stop=(k == 3))
                    last.then_inc(u_done, 1)
                if inside(i, j - 2, 2, NW):
                    pe.wait_ge(agg_ready, s - 1)
                    if looped or s >= 3:
                        pe.wait_ge(at_ready, s - 2)
                    for k in range(2):
                        last = nc.tensor.transpose(pR[:, k * P:(k + 1) * P], agg[:, j, k * P:(k + 1) * P],
                                                   keep.ident[:, :])
                    last.then_inc(at_done, 1)
                if inside(i, j - 1, 2, NW):
                    b = (j - 1) % 2
                    pe.wait_ge(st_ready, s)
                    if looped or s >= 2:
                        pe.wait_ge(agg_ready, s - 1)
                    for k in range(4):
                        last = mm(pG[:, 0:D], sT[:, b, k * P:(k + 1) * P], mw2[:, k, :], start=(k == 0), stop=(k == 3))
                    last.then_inc(agg_done, 1)
                if inside(i, j, 2, NW):
                    pe.wait_ge(s_copied, s + 1)
                    if looped or s >= 2:
                        pe.wait_ge(st_ready, s - 1)
                    for k in range(4):
                        last = nc.tensor.transpose(pS[j][:, k * P:(k + 1) * P],
                                                   s_win[:, j, k * P:(k + 1) * P], keep.ident[:, :])
                    last.then_inc(st_done, 1)

            walk(pe, step)

        @block.scalar
        def _(act):
            def step(i, j):
                s = 2 * i + j
                looped = not isinstance(i, int)
                if inside(i, j - 3, 2, NW):
                    b = (j - 3) % 2
                    act.wait_ge(u_done, s - 2)
                    if looped or s >= 5:
                        act.wait_ge(x_done, s - 4)
                    for m in range(4):
                        nc.scalar.activation(uT[:, b, m * P:(m + 1) * P], pU[b][:, m * P:(m + 1) * P], ACT.Relu,
                                             bias=ub1[:, m:m + 1]).then_inc(u_ready, 1)
                if inside(i, j - 2, 2, NW):
                    act.wait_ge(at_done, s - 1)
                    if looped or s >= 4:
                        act.wait_ge(u_done, s - 3)
                    nc.scalar.copy(aggT[:, j, :], pR[:, 0:D]).then_inc(at_ready, 1)
                if inside(i, j, 2, NW):
                    act.wait_ge(st_done, s + 1)
                    if looped or s >= 2:
                        act.wait_ge(agg_done, s - 1)
                    nc.scalar.copy(sT[:, j, :], pS[j][:, :]).then_inc(st_ready, 1)

            act.wait_ge(w_in, 16 * 9)
            walk(act, step)
            act.wait_ge(var_ready, 1)
            nc.scalar.activation(std[:, :], std[:, :], ACT.Sqrt).then_inc(std_ready, 1)

        @block.vector
        def _(dve):
            v = nc.vector
            dve.wait_ge(w_in, 16 * 9)

            def step(i, j):
                s = 2 * i + j
                looped = not isinstance(i, int)
                if inside(i, j - 4, 2, NW):
                    dve.wait_ge(x_done, s - 3)
                    if looped or s >= 5:
                        dve.wait_ge(x_ready, s - 4)
                    r = keep.resid[:, bass.ds(s - 4, 1), :].rearrange("p w d -> p (w d)")
                    v.tensor_tensor(xm[:, :], pX[j][:, 0:D], ub2[:, :], ALU.add).then_inc(xm_ready, 1)
                    dve.wait_ge(xm_ready, s - 3)
                    v.tensor_tensor(r, r, xm[:, :], ALU.add).then_inc(x_ready, 1)
                    dve.wait_ge(x_ready, s - 3)
                    v.bn_stats(stats[:, bass.ds(s - 4, 1), :].rearrange("p w c -> p (w c)"), r).then_inc(stat_ready, 1)
                if inside(i, j - 1, 2, NW):
                    b = (j - 1) % 2
                    dve.wait_ge(agg_done, s)
                    if looped or s >= 3:
                        dve.wait_ge(at_done, s - 2)
                    v.scalar_tensor_tensor(out=agg[:, b, :], in0=mb2[:, :], scalar=keep.deg_src[:, bass.ds(s - 1, 1)],
                                           in1=pG[:, 0:D], op0=ALU.mult, op1=ALU.add).then_inc(agg_ready, 1)

            walk(dve, step)
            dve.wait_ge(stat_ready, NW)
            link = Chain(dve, own)
            for w in range(NW):
                link(v.bn_aggr(mv[:, w, :], stats[:, w, :]))
            v.tensor_scalar(std[:, :], mv[:, :, 1], EPS, None, ALU.add).then_inc(var_ready, 1)
            dve.wait_ge(std_ready, 1)
            link(v.reciprocal(keep.rstd[:, :], std[:, :]))
            link(v.scalar_tensor_tensor(out=keep.nmr[:, :], in0=mv[:, :, 0], scalar=-1.0, in1=keep.rstd[:, :],
                                        op0=ALU.mult, op1=ALU.mult))


def project(nc, io, dr, keep, layer):
    with ExitStack() as stack:
        g = Names(nc, stack)
        w = g.sb(f"w_{layer}", [P, 2, D])
        bias = g.sb(f"bias_{layer}", [P, D])
        z = g.sb(f"z_{layer}", [P, 2, D])
        h = g.sb(f"h_{layer}", [P, 2, D])
        hT = g.sb(f"hT_{layer}", [P, 2, D])
        pT = [g.ps(f"pT_{layer}_{n}", [P, HID]) for n in range(2)]
        pY = [g.ps(f"pY_{layer}_{n}", [P, HID]) for n in range(2)]
        w_in = g.sem(f"w_in_{layer}")
        z_ready = g.sem(f"z_ready_{layer}")
        h_ready = g.sem(f"h_ready_{layer}")
        tr_done = g.sem(f"tr_done_{layer}")
        ht_ready = g.sem(f"ht_ready_{layer}")
        y_done = g.sem(f"y_done_{layer}")
        y_ready = g.sem(f"y_ready_{layer}")
        y_out = g.sem(f"y_out_{layer}")
        pairs_in = g.sem(f"pairs_in_{layer}")

        def walk(eng, body):
            blocks(eng, NW + 3, 2, 2, NW // 2, body)

        block = stack.enter_context(nc.Block())

        @block.sync
        def _(sp):
            sp.dma_start(w[:, :, :], io[f"L1_gnn_W{layer}"].rearrange("(k p) n -> p k n", p=P)).then_inc(w_in, 16)
            if layer > 1:
                sp.dma_start(bias[:, :], io[f"L1_gnn_b{layer - 1}"].partition_broadcast(P)).then_inc(w_in, 16)
            else:
                sp.dma_start(keep.pairs[:, :, :], dr.dst_list[:, :, :]).then_inc(pairs_in, 16)

            def step(i, j):
                s = 2 * i + j
                if inside(i, j - 3, 2, NW):
                    sp.wait_ge(y_ready, s - 2)
                    sp.dma_start(dr.Y[bass.ds((s - 3) * P, P), :], keep.acc[:, bass.ds((s - 3) * D, D)]
                                 ).then_inc(y_out, 16)

            walk(sp, step)
            sp.wait_ge(y_out, 16 * NW)
            if layer == 1:
                sp.wait_ge(pairs_in, 16)

        @block.vector
        def _(dve):
            v = nc.vector
            dve.wait_ge(w_in, 16 * (1 + (layer > 1)))

            def step(i, j):
                s = 2 * i + j
                looped = not isinstance(i, int)
                if layer > 1 and inside(i, j, 2, NW):
                    if looped or s >= 2:
                        dve.wait_ge(h_ready, s - 1)
                    v.scalar_tensor_tensor(out=z[:, j, :], in0=keep.acc[:, bass.ds(s * D, D)],
                                           scalar=keep.dis[:, bass.ds(s, 1)], in1=bias[:, :],
                                           op0=ALU.mult, op1=ALU.add).then_inc(z_ready, 1)
                if inside(i, j - 3, 2, NW):
                    dve.wait_ge(y_done, s - 2)
                    v.tensor_scalar(keep.acc[:, bass.ds((s - 3) * D, D)], pY[(j - 3) % 2][:, 0:D],
                                    keep.dis[:, bass.ds(s - 3, 1)], None, ALU.mult).then_inc(y_ready, 1)

            walk(dve, step)

        @block.scalar
        def _(act):
            def step(i, j):
                s = 2 * i + j
                looped = not isinstance(i, int)
                if inside(i, j, 2, NW):
                    if looped or s >= 2:
                        act.wait_ge(tr_done, s - 1)
                    if layer == 1:
                        nc.scalar.activation(h[:, j, :], keep.resid[:, bass.ds(s, 1), :].rearrange("p w d -> p (w d)"),
                                             ACT.Relu, bias=keep.nmr[:, bass.ds(s, 1)],
                                             scale=keep.rstd[:, bass.ds(s, 1)]).then_inc(h_ready, 1)
                    else:
                        act.wait_ge(z_ready, s + 1)
                        nc.scalar.activation(h[:, j, :], z[:, j, :], ACT.Gelu_apprx_tanh).then_inc(h_ready, 1)
                if inside(i, j - 1, 2, NW):
                    b = (j - 1) % 2
                    act.wait_ge(tr_done, s)
                    if looped or s >= 3:
                        act.wait_ge(y_done, s - 2)
                    nc.scalar.copy(hT[:, b, :], pT[b][:, 0:D]).then_inc(ht_ready, 1)

            walk(act, step)

        @block.tensor
        def _(pe):
            pe.wait_ge(w_in, 16 * (1 + (layer > 1)))

            def step(i, j):
                s = 2 * i + j
                looped = not isinstance(i, int)
                if inside(i, j, 2, NW):
                    pe.wait_ge(h_ready, s + 1)
                    if looped or s >= 2:
                        pe.wait_ge(ht_ready, s - 1)
                    for k in range(2):
                        last = nc.tensor.transpose(pT[j][:, k * P:(k + 1) * P], h[:, j, k * P:(k + 1) * P],
                                                   keep.ident[:, :])
                    last.then_inc(tr_done, 1)
                if inside(i, j - 1, 2, NW):
                    b = (j - 1) % 2
                    pe.wait_ge(ht_ready, s)
                    if looped or s >= 3:
                        pe.wait_ge(y_ready, s - 2)
                    for k in range(2):
                        last = nc.tensor.matmul(pY[b][:, 0:D], hT[:, b, k * P:(k + 1) * P], w[:, k, :],
                                                start=(k == 0), stop=(k == 1))
                    last.then_inc(y_done, 1)

            walk(pe, step)


def spread(nc, io, dr, keep, layer):
    with ExitStack() as stack:
        g = Names(nc, stack)
        R = 8
        LAG = 6
        rows = g.sb(f"rows_{layer}", [P, R, D])
        index = g.sb(f"index_{layer}", [P, 4, 2], I32)
        onehot = g.sb(f"onehot_{layer}", [P, R, P])
        pN = [g.ps(f"pN_{layer}_{n}", [P, HID]) for n in range(4)]
        index_ready = g.sem(f"index_ready_{layer}")
        oh_ready = g.sem(f"oh_ready_{layer}")
        rows_in = [g.sem(f"rows_in_{layer}_{n}") for n in range(R)]
        node_done = g.sem(f"node_done_{layer}")
        added = g.sem(f"added_{layer}")
        pairs_i = keep.pairs_i
        LAST = NT // U - 1

        block = stack.enter_context(nc.Block())

        @block.gpsimd
        def _(pool):
            turn = g.sem(f"turn_{layer}")

            def step(i, j):
                t = U * i + j
                if j % 2 == 0:
                    pool.wait_ge(index_ready, (U // 2) * i + j // 2 + 1)
                if not isinstance(i, int) or t >= R:
                    pool.wait_ge(node_done, t - R + 1)
                hold(pool, turn)
                nc.gpsimd.indirect_dma_start(
                    rows[:, j, :], None, dr.Y,
                    bass.IndirectOffsetOnAxis(ap=index[:, j // 2, j % 2:j % 2 + 1], axis=0)).then_inc(rows_in[j], 16)

            blocks(pool, NT, U, 1, LAST, step)

        @block.tensor
        def _(pe):
            def step(i, j):
                t = U * i + j
                pe.wait_ge(oh_ready, t + 1)
                pe.wait_ge(rows_in[j], 16 * (i + 1))
                if not isinstance(i, int) or t >= 4:
                    pe.wait_ge(added, t - 3)
                nc.tensor.matmul(pN[j % 4][:, 0:D], onehot[:, j, :], rows[:, j, :], start=True, stop=True
                                 ).then_inc(node_done, 1)

            blocks(pe, NT, U, 1, LAST, step)

        @block.vector
        def _(dve):
            v = nc.vector

            def step(i, j):
                t = U * i + j
                if inside(i, j, U, NT):
                    if j % 2 == 0:
                        v.tensor_copy(index[:, j // 2, :], pairs_i[:, bass.ds(t, 2), 0]).then_inc(index_ready, 1)
                    v.tensor_scalar(onehot[:, j, :], keep.iota[:, :], keep.pairs[:, bass.ds(t, 1), 1:2].rearrange(
                        "p t w -> p (t w)"), None, ALU.is_equal).then_inc(oh_ready, 1)
                if inside(i, j - LAG, U, NT):
                    dve.wait_ge(node_done, t - LAG + 1)
                    if not isinstance(i, int) or t > LAG:
                        dve.wait_ge(added, t - LAG)
                    w = dve.value_load(keep.dst_map[0:1, bass.ds(t - LAG, 1)], min_val=0, max_val=NW - 1)
                    sw = keep.acc[:, bass.ds(w * D, D)]
                    v.tensor_tensor(sw, sw, pN[(j - LAG) % 4][:, 0:D], ALU.add).then_inc(added, 1)

            blocks(dve, NT + LAG, U, 1, LAST, step)


def finish(nc, io, dr, keep, out):
    with ExitStack() as stack:
        g = Names(nc, stack)
        bias = g.sb("bias_out", [P, D])
        b_in = g.sem("b_in_out")
        own = g.sem("own_out")
        res = g.sem("res_out")
        stored = g.sem("stored")
        block = stack.enter_context(nc.Block())

        @block.sync
        def _(sp):
            sp.dma_start(bias[:, :], io["L1_gnn_b3"].partition_broadcast(P)).then_inc(b_in, 16)
            for w in range(NW):
                sp.wait_ge(res, w + 1)
                n = P if w < NW - 1 else TAIL
                sp.dma_start(out[w * P:w * P + n, :], keep.resid[0:n, w, :]).then_inc(stored, 16)
            sp.wait_ge(stored, 16 * NW)

        @block.vector
        def _(dve):
            v = nc.vector
            dve.wait_ge(b_in, 16)
            for w in range(NW):
                a = keep.acc[:, w * D:(w + 1) * D]
                v.scalar_tensor_tensor(out=a, in0=a, scalar=keep.dis[:, w:w + 1], in1=bias[:, :],
                                       op0=ALU.mult, op1=ALU.add).then_inc(own, 1)
                dve.wait_ge(own, w + 1)
                v.tensor_tensor(keep.resid[:, w, :], keep.resid[:, w, :], a, ALU.add).then_inc(res, 1)


class Store:
    pass


def build(nc, io, out):
    dr, keep = Store(), Store()
    with ExitStack() as stack:
        g = Names(nc, stack)
        dr.src_list = nc.dram_tensor("src_list", [P, LT, ROW], F32).ap()
        dr.dst_list = nc.dram_tensor("dst_list", [P, LT, 2], F32).ap()
        dr.feat = nc.dram_tensor("feat_rows", [COLS * P, EF], F32).ap()
        dr.hT = nc.dram_tensor("hT_rows", [NW, P, D], F32).ap()
        dr.B = nc.dram_tensor("B_rows", [NPAD, HID], F32).ap()
        dr.Y = nc.dram_tensor("Y_rows", [NPAD, D], F32).ap()
        keep.resid = g.sb("resid", [P, NW, D])
        keep.iota = g.sb("iota", [P, P])
        keep.iota16 = g.sb("iota16", [P, P], BF16)
        keep.ident = g.sb("ident", [P, P])
        keep.ident16 = g.sb("ident16", [P, P], BF16)
        keep.dis = g.sb("dis", [P, NW])
        keep.deg_src = g.sb("deg_src", [P, NW])
        keep.rstd = g.sb("rstd_k", [P, NW])
        keep.nmr = g.sb("nmr_k", [P, NW])
        keep.src_map = g.sb("src_map", [1, NT], I32)
        keep.dst_map = g.sb("dst_map", [1, NT], I32)
        with ExitStack() as inner:
            k = Names(nc, inner)
            keep.A = k.sb("A", [P, 3, NW * HID], BF16)
            keep.row_dst = k.sb("row_dst", [P, COLS], I32)
            pair = k.sb("pair", [P, LT * 2])
            keep.pair_w = pair[:, :].rearrange("p (t w) -> p t w", w=2)
            keep.pair_flat = pair
            keep.pair = keep.pair_w[:, 0:COLS, :]
            keep.pair_i = pair[:, :].bitcast(I32).rearrange("p (t w) -> p t w", w=2)[:, 0:COLS, :]
            keep.we = k.sb("we_rows", [EW, HID], BF16)
            sort_and_embed(nc, io, dr, keep)
            with ExitStack() as high:
                keep.S = Names(nc, high).sb("S", [P, NW * HID])
                edge_mlp(nc, io, dr, keep)
                node_mlp(nc, io, dr, keep)
        keep.acc = g.sb("acc", [P, NW * D])
        pairs = g.sb("pairs", [P, LT * 2])
        keep.pairs = pairs[:, :].rearrange("p (t w) -> p t w", w=2)
        keep.pairs_i = pairs[:, :].bitcast(I32).rearrange("p (t w) -> p t w", w=2)
        for layer in (1, 2, 3):
            project(nc, io, dr, keep, layer)
            spread(nc, io, dr, keep, layer)
        finish(nc, io, dr, keep, out)


_INS = ["x", "src", "dst", "edge_attr_16", "L0_gnn_mW1", "L0_gnn_mb1", "L0_gnn_mW2", "L0_gnn_mb2", "L0_gnn_uW1",
        "L0_gnn_ub1", "L0_gnn_uW2", "L0_gnn_ub2", "L1_gnn_W1", "L1_gnn_b1", "L1_gnn_W2", "L1_gnn_b2", "L1_gnn_W3",
        "L1_gnn_b3"]


def kernel(**inputs):
    import numpy as _np
    import concourse.bacc as _bacc
    from concourse import mybir as _mybir
    from concourse.bass_utils import run_bass_kernel_spmd as _run

    nc = _bacc.Bacc("TRN2", target_bir_lowering=False, num_devices=1)
    arrays, io = {}, {}
    for name in _INS:
        a = _np.ascontiguousarray(inputs[name])
        arrays[f"in_{name}_dram"] = a
        io[name] = nc.dram_tensor(f"in_{name}_dram", a.shape, _mybir.dt.from_np(a.dtype), kind="ExternalInput").ap()
    out = nc.dram_tensor("out_0_dram", (N, D), _mybir.dt.float32, kind="ExternalOutput").ap()
    build(nc, io, out)
    r = _run(nc, [arrays], core_ids=[0])
    return r.results[0]["out_0_dram"]
```

```python
from contextlib import ExitStack

import concourse.bass as bass
from concourse import mybir

P = 128
ALU = mybir.AluOpType
ACT = mybir.ActivationFunctionType
AX = mybir.AxisListType
F32 = mybir.dt.float32
BF16 = mybir.dt.bfloat16
I32 = mybir.dt.int32

N = 3125
E = 50000
D = 256
HID = 512
EF = 16
NW = -(-N // P)
NPAD = NW * P
TAIL = N - (NW - 1) * P
EPS = 1e-5

CH = 7
COLS = 392
FULLP = E // COLS
LASTC = E - FULLP * COLS
PADKEY = NW * P
BINS = NW + 1
NT = -(-E // P) + NW
LT = NT + 2
HALVES = COLS // (2 * CH)
SPLITS = 6
ROW = 2 + SPLITS * EF // 2
EW = SPLITS * EF

GATHERS = 16
LC = 4
assert COLS * P >= E + 0 and COLS * P - E <= 2 * P and HALVES * 2 * CH == COLS and NT % GATHERS == 0


def blocks(eng, count, unroll, lo, hi, body):
    for i in range(lo):
        for j in range(unroll):
            body(i, j)
    with eng.Fori(lo, hi) as i:
        for j in range(unroll):
            body(i, j)
    for i in range(hi, -(-count // unroll)):
        for j in range(unroll):
            if i * unroll + j < count:
                body(i, j)


def inside(i, j, unroll, n):
    return not isinstance(i, int) or 0 <= i * unroll + j < n


def windows(nc, eng, tile_map, i, lag, unroll):
    first, skip, n = i * unroll - lag, 0, unroll
    if isinstance(i, int):
        skip = max(0, -first)
        n = min(NT, first + unroll) - first - skip
        first += skip
    if n <= 0:
        return {}
    _, got = nc.values_load_multi_w_load_instructions(
        tile_map[0:1, bass.ds(first, n)], engines=[eng.engine], min_val=0, max_val=NW - 1,
        skip_runtime_bounds_check_because="the map counts at most NW - 1 windows before a tile")
    return {skip + k: w for k, w in enumerate(got)}


def hold(pool, turn):
    pool.sem_inc(turn, 1)


class Names:

    def __init__(self, nc, stack):
        self.nc, self.stack = nc, stack

    def sb(self, name, shape, dt=F32):
        return self.stack.enter_context(self.nc.sbuf_tensor(name, shape, dt))

    def ps(self, name, shape, dt=F32):
        return self.stack.enter_context(self.nc.psum_tensor(name, shape, dt))

    def sem(self, name):
        return self.stack.enter_context(self.nc.semaphore(name))


class Chain:

    def __init__(self, eng, sem):
        self.eng, self.sem, self.n = eng, sem, 0

    def __call__(self, ins):
        self.n += 1
        ins.then_inc(self.sem, 1)
        self.eng.wait_ge(self.sem, self.n)


def sort_and_embed(nc, io, dr, keep):
    with ExitStack() as stack:
        g = Names(nc, stack)
        key = [g.sb(f"key{n}", [P, COLS], I32) for n in range(2)]
        key_hi = g.sb("key_hi", [P, COLS], I32)
        key_lo_w = g.sb("key_lo", [P, LT], I32)
        key_lo = key_lo_w[:, 0:COLS]
        hi16 = g.sb("hi16", [P, COLS], BF16)
        lo16 = [g.sb(f"lo16_{n}", [P, COLS], BF16) for n in range(2)]
        onehot_hi = [g.sb(f"onehot_hi{n}", [P, BINS, COLS], BF16) for n in range(2)]
        count = keep.A[:, 3 * NW * HID - 2 * BINS * COLS:3 * NW * HID].bitcast(F32)
        count3 = count.rearrange("p (b t) -> p b t", b=BINS)
        posf_w = g.sb("posf", [P, LT])
        posf = posf_w[:, 0:COLS]
        posi, pos_lo = key_hi, key_lo
        row_src = g.sb("row_src", [P, COLS], I32)
        tot = g.sb("tot", [P, BINS])
        before = g.sb("before", [P, BINS])
        tiles_i = g.sb("tiles_i", [P, NW], I32)
        tiles_f = g.sb("tiles_f", [P, NW])
        tiles_end = [g.sb(f"tiles_end{n}", [P, NW]) for n in range(2)]
        end_diag = g.sb("end_diag", [NW, NW])
        end_col = g.sb("end_col", [NW, 1])
        start = g.sb("start", [P, BINS])
        offset = g.sb("offset", [P, BINS])
        tile_no = key_lo_w[:, 0:NT]
        tile_nof = g.sb("tile_nof", [P, NT])
        ended = posf_w[0:NW - 1, 0:NT]
        feat = g.sb("feat", [P, 2, 2 * CH, EF])
        ring = g.sb("ring", [P, 2, CH, ROW])
        ring16 = ring[:, :, :, :].rearrange("p s t w -> p (s t w)").bitcast(BF16).rearrange(
            "p (s t w) -> p s t w", s=2, t=CH)
        ring_i = ring[:, :, :, :].rearrange("p s t w -> p (s t w)").bitcast(I32).rearrange(
            "p (s t w) -> p s t w", s=2, t=CH)
        ring_row = g.sb("ring_row", [P, 2, CH], I32)
        rest = g.sb("rest", [P, 2, CH, EF])
        FR = 11
        fill = g.sb("fill", [P, FR, ROW])
        fill_d = keep.pair_w
        assert LT % FR == 0
        iota_i = g.sb("iota_i", [P, P], I32)
        part_i = g.sb("part_i", [P, 1], I32)
        part = g.sb("part", [P, 1])
        before_m = g.sb("before_m", [P, P])
        ones = g.sb("ones", [P, P])
        onehot_lo = g.sb("onehot_lo", [P, 4, CH, P], BF16)
        stats = g.sb("stats", [P, NW, 6])
        mv = g.sb("mv", [P, NW, 2])
        std = g.sb("std", [P, NW])
        rstd = g.sb("rstd", [P, NW])
        nmr = g.sb("nmr", [P, NW])
        h = g.sb("h", [P, 2, D])
        hT = g.sb("hT", [P, 2, D])
        w1 = g.sb("w1", [P, 4, HID])
        b1 = g.sb("b1", [P, HID])
        vA = g.sb("vA", [P, HID])
        rA = g.sb("rA", [P, HID])
        bst = g.sb("bst", [P, 2, HID])
        we, we_r = vA[0:EF, :], rA[0:EF, :]
        we_part = [bst[0:EF, :, :].rearrange("p s n -> p (s n)").bitcast(BF16)[:, n * HID:(n + 1) * HID]
                   for n in range(3)]
        pA = [g.ps(f"pA{n}", [P, HID]) for n in range(2)]
        pB = [g.ps(f"pB{n}", [P, HID]) for n in range(2)]
        pT = [g.ps(f"pT{n}", [P, HID]) for n in range(2)]
        pH = [g.ps(f"pH{n}", [P, HID]) for n in range(2)]
        sum_before, sum_all = pT[1][:, 0:BINS], pT[1][:, 32:32 + BINS]
        PLACE = 3

        keys_set = g.sem("keys_set")
        keys_in = g.sem("keys_in")
        x_in = g.sem("x_in")
        feat_whole = g.sem("feat_whole")
        feat_in = [g.sem(f"feat_in{n}") for n in range(2)]
        w_in = g.sem("w_in")
        x_zero = g.sem("x_zero")
        iota_ready = g.sem("iota_ready")
        fill_ready = g.sem("fill_ready")
        fill_part = g.sem("fill_part")
        filled = g.sem("filled")
        own = g.sem("dve_own")
        consts = g.sem("consts")
        tot_ready = g.sem("tot_ready")
        sums_done = g.sem("sums_done")
        sums_used = g.sem("sums_used")
        end_ready = g.sem("end_ready")
        map_done = g.sem("map_done")
        var_ready = g.sem("var_ready")
        std_ready = g.sem("std_ready")
        ln_ready = g.sem("ln_ready")
        payload = g.sem("payload")
        scattered = [g.sem(f"scattered{n}") for n in range(2)]
        oh_ready = g.sem("oh_ready")
        hist_done = g.sem("hist_done")
        h_ready = g.sem("h_ready")
        resid_done = g.sem("resid_done")
        trh_done = g.sem("trh_done")
        ht_ready = g.sem("ht_ready")
        ht_out = [g.sem(f"ht_out{n}") for n in range(2)]
        ab_done = g.sem("ab_done")
        va_ready = g.sem("va_ready")
        a_hi = g.sem("a_hi")
        ra_ready = g.sem("ra_ready")
        a_mid = g.sem("a_mid")
        a_lo = g.sem("a_lo")
        b_ready = g.sem("b_ready")
        b_out = [g.sem(f"b_out{n}") for n in range(2)]
        deg_ready = g.sem("deg_ready")
        sq_ready = g.sem("sq_ready")
        we_parts = g.sem("we_parts")
        we_out = g.sem("we_out")

        def a_part(w, k):
            return keep.A[:, bass.ds(w * (3 * HID) + k * HID, HID)]

        def walk(eng, body):
            blocks(eng, HALVES, 2, 3, NW // 2, body)

        block = stack.enter_context(nc.Block())

        @block.sync
        def _(sp):
            sp.wait_ge(keys_set, 2)
            for n, a in enumerate((io["src"], io["dst"])):
                sp.dma_start(key[n][0:FULLP, :], a[0:FULLP * COLS].rearrange("(p t) -> p t", t=COLS)
                             ).then_inc(keys_in, 16)
                sp.dma_start(key[n][FULLP:FULLP + 1, 0:LASTC],
                             a[FULLP * COLS:E].rearrange("(p t) -> p t", p=1)).then_inc(keys_in, 16)
            sp.wait_ge(x_zero, 1)
            sp.dma_start(keep.resid[:, 0:NW - 1, :], io["x"][0:(NW - 1) * P, :].rearrange("(w p) d -> p w d", p=P)
                         ).then_inc(x_in, 16)
            sp.dma_start(keep.resid[0:TAIL, NW - 1, :], io["x"][(NW - 1) * P:N, :]).then_inc(x_in, 16)
            sp.dma_start(w1[:, :, :], io["L0_gnn_mW1"][0:2 * D, :].rearrange("(k p) n -> p k n", p=P)
                         ).then_inc(w_in, 16)
            sp.dma_start(we[:, :], io["L0_gnn_mW1"][2 * D:2 * D + EF, :]).then_inc(w_in, 16)
            sp.dma_start(b1[:, :], io["L0_gnn_mb1"].partition_broadcast(P)).then_inc(w_in, 16)
            sp.wait_ge(fill_ready, 4)
            for n in range(LT // FR):
                sp.dma_start(dr.src_list[:, n * FR:(n + 1) * FR, :], fill[:, :, :]).then_inc(filled, 16)
            sp.dma_start(dr.dst_list[:, :, :], fill_d[:, :, :]).then_inc(filled, 16)

            feat_rows = dr.feat.rearrange("(p t) f -> p (t f)", t=COLS)

            def load_feat(i, j):
                s = 2 * i + j
                if not isinstance(i, int) or s >= 2:
                    sp.wait_ge(payload, 14 * (s - 1))
                sp.dma_start(feat[:, j, :, :].rearrange("p t f -> p (t f)"),
                             feat_rows[:, bass.ds(s * 2 * CH * EF, 2 * CH * EF)]).then_inc(feat_in[j], 16)

            def step(i, j):
                load_feat(i, j)
                if isinstance(i, int) and 2 * i + j == 1:
                    sp.wait_ge(we_parts, 1)
                    for r, which in enumerate((0, 1, 2, 0, 1, 0)):
                        sp.dma_start(keep.we[r * EF:(r + 1) * EF, :], we_part[which][:, :]).then_inc(we_out, 16)
                if inside(i, j - 1, 2, NW):
                    sp.wait_ge(ht_ready, 2 * i + j)
                    sp.dma_start(dr.hT[bass.ds(2 * i + j - 1, 1), :, :].rearrange("w p n -> p (w n)"),
                                 hT[:, (j - 1) % 2, :]).then_inc(ht_out[(j - 1) % 2], 16)
                if inside(i, j - 2, 2, NW):
                    sp.wait_ge(b_ready, 2 * i + j - 1)
                    sp.dma_start(dr.B[bass.ds((2 * i + j - 2) * P, P), :], bst[:, j % 2, :]
                                 ).then_inc(b_out[j % 2], 16)

            sp.wait_ge(feat_whole, 48)
            walk(sp, step)
            sp.wait_ge(we_out, 16 * SPLITS)
            for q in ht_out:
                sp.wait_ge(q, 16 * (NW // 2))
            sp.wait_ge(ht_out[0], 16 * (NW - NW // 2))
            sp.wait_ge(b_out[0], 16 * (NW - NW // 2))
            sp.wait_ge(b_out[1], 16 * (NW // 2))

        @block.gpsimd
        def _(pool):
            turn = keep.turn
            for n in range(2):
                nc.gpsimd.memset(key[n][:, :], PADKEY).then_inc(keys_set, 1)
            nc.gpsimd.memset(keep.resid[:, NW - 1, :], 0.0).then_inc(x_zero, 1)
            nc.gpsimd.iota(iota_i[:, :], [[1, P]], base=0, channel_multiplier=0).then_inc(iota_ready, 1)
            nc.gpsimd.iota(part_i[:, :], [[0, 1]], base=0, channel_multiplier=1).then_inc(iota_ready, 1)
            nc.gpsimd.iota(tile_no[:, :], [[1, NT]], base=0, channel_multiplier=0).then_inc(iota_ready, 1)
            nc.gpsimd.memset(fill[:, :, :], 0.0).then_inc(fill_part, 1)
            nc.gpsimd.memset(fill_d[:, :, :], 0.0).then_inc(fill_part, 1)
            pool.wait_ge(fill_part, 2)
            pool.wait_ge(feat_whole, 48)
            nc.gpsimd.memset(fill[:, :, 0:1], -1.0).then_inc(fill_ready, 2)
            nc.gpsimd.memset(fill_d[:, :, 1:2], -1.0).then_inc(fill_ready, 2)
            pool.wait_ge(filled, 16 * (LT // FR + 1))
            with pool.Fori(0, HALVES) as i:
                for c in range(2):
                    pool.wait_ge(payload, i * 14 + 7 * c + 7)
                    hold(pool, turn)
                    for t in range(CH):
                        nc.gpsimd.indirect_dma_start(
                            dr.src_list[:, :, :].rearrange("p t w -> (p t) w"),
                            bass.IndirectOffsetOnAxis(ap=ring_row[:, c, t:t + 1], axis=0),
                            ring[:, c, t, :], None).then_inc(scattered[c], 16)
            for q in scattered:
                pool.wait_ge(q, 16 * CH * HALVES)

        @block.scalar
        def _(act):
            act.dma_start(dr.feat[0:E, :].rearrange("(p t) f -> p (t f)", t=E // 16),
                          io["edge_attr_16"].rearrange("(p t) f -> p (t f)", t=E // 16)).then_inc(feat_whole, 16)
            act.wait_ge(fill_part, 2)
            act.dma_start(dr.feat[E:E + P, :], fill[:, 0, 0:EF]).then_inc(feat_whole, 16)
            act.dma_start(dr.feat[E + P:COLS * P, :], fill[0:COLS * P - E - P, 0, 0:EF]).then_inc(feat_whole, 16)
            act.wait_ge(var_ready, 1)
            nc.scalar.activation(std[:, :], std[:, :], ACT.Sqrt).then_inc(std_ready, 1)
            act.wait_ge(ln_ready, 2)

            def step(i, j):
                s = 2 * i + j
                if inside(i, j, 2, NW):
                    if not isinstance(i, int) or s >= 2:
                        act.wait_ge(trh_done, s - 1)
                        act.wait_ge(resid_done, s - 1)
                    nc.scalar.activation(h[:, j, :], keep.resid[:, bass.ds(s, 1), :].rearrange("p w d -> p (w d)"),
                                         ACT.Relu, bias=nmr[:, bass.ds(s, 1)], scale=rstd[:, bass.ds(s, 1)]
                                         ).then_inc(h_ready, 1)
                if inside(i, j - 1, 2, NW):
                    b = (j - 1) % 2
                    act.wait_ge(trh_done, s)
                    if not isinstance(i, int) or s >= 3:
                        act.wait_ge(ab_done, s - 2)
                        act.wait_ge(ht_out[b], 16 * (i + (j - 1) // 2))
                    nc.scalar.copy(hT[:, b, :], pT[b][:, 0:D]).then_inc(ht_ready, 1)
                if inside(i, j - 2, 2, NW):
                    act.wait_ge(va_ready, s - 1)
                    nc.scalar.copy(a_part(s - 2, 0), vA[:, :]).then_inc(a_hi, 1)
                    act.wait_ge(ab_done, s - 1)
                    if not isinstance(i, int) or s >= 4:
                        act.wait_ge(b_out[j], 16 * (i - 1))
                    if isinstance(i, int) and s == 2:
                        act.wait_ge(we_out, 16 * SPLITS)
                    nc.scalar.copy(bst[:, j, :], pB[j][:, :]).then_inc(b_ready, 1)
                    act.wait_ge(ra_ready, s - 1)
                    nc.scalar.copy(a_part(s - 2, 1), rA[:, :]).then_inc(a_mid, 1)

            walk(act, step)
            act.wait_ge(deg_ready, 2)
            nc.scalar.activation(keep.dis[:, :], keep.dis[:, :], ACT.Sqrt).then_inc(sq_ready, 1)

        @block.vector
        def _(dve):
            v = nc.vector
            link = Chain(dve, own)
            dve.wait_ge(iota_ready, 3)
            link(v.tensor_copy(keep.iota[:, :], iota_i[:, :]))
            link(v.tensor_copy(part[:, :], part_i[:, :]))
            v.tensor_copy(keep.iota16[:, :], keep.iota[:, :]).then_inc(consts, 1)
            v.tensor_scalar(keep.ident[:, :], keep.iota[:, :], part[:, 0:1], None, ALU.is_equal).then_inc(consts, 1)
            v.tensor_scalar(keep.ident16[:, :], keep.iota[:, :], part[:, 0:1], None, ALU.is_equal).then_inc(consts, 1)
            v.tensor_scalar(before_m[:, :], keep.iota[:, :], part[:, 0:1], None, ALU.is_gt).then_inc(consts, 1)
            v.memset(ones[:, :], 1.0).then_inc(consts, 1)
            v.tensor_copy(tile_nof[:, :], tile_no[:, :]).then_inc(consts, 1)
            dve.wait_ge(consts, 6)

            def many(count, op):
                for b in range(count):
                    op(b).then_inc(own, 1)
                link.n += count
                dve.wait_ge(own, link.n)

            def find_bins(n):
                link(v.tensor_scalar(key_hi[:, :], key[n][:, :], 7, None, ALU.arith_shift_right))
                link(v.tensor_scalar(key_lo[:, :], key[n][:, :], P - 1, None, ALU.bitwise_and))
                link(v.tensor_copy(hi16[:, :], key_hi[:, :]))
                link(v.tensor_copy(lo16[n][:, :], key_lo[:, :]))
                many(BINS, lambda b: v.tensor_scalar(onehot_hi[n][:, b, :], hi16[:, :], float(b), None, ALU.is_equal))

            def count_bins(n, b0, b1):
                flat = onehot_hi[n][:, b0:b1, :].rearrange("p b t -> p (b t)")
                first = count[:, b0 * COLS - 1:b0 * COLS] if b0 else 0.0
                link(v.tensor_tensor_scan(count[:, b0 * COLS:b1 * COLS], flat, flat, first, ALU.add, ALU.max))

            def total_bins(n):
                link(v.tensor_copy(tot[:, :], count3[:, :, COLS - 1]))
                v.tensor_tensor(tot[:, 1:BINS], tot[:, 1:BINS], count3[:, 0:BINS - 1, COLS - 1], ALU.subtract
                                ).then_inc(tot_ready, 1)

            def start_bins(n):
                dve.wait_ge(sums_done, n + 1)
                link(v.tensor_scalar(tiles_i[:, :], sum_all[:, 0:NW], float(P - 1), None, ALU.add))
                v.tensor_copy(before[:, :], sum_before).then_inc(sums_used, 1)
                link(v.tensor_scalar(tiles_i[:, :], tiles_i[:, :], 7, None, ALU.arith_shift_right))
                link(v.tensor_copy(tiles_f[:, :], tiles_i[:, :]))
                link(v.tensor_tensor_scan(tiles_end[n][:, :], tiles_f[:, :], tiles_f[:, :], 0.0, ALU.add, ALU.max))
                link(v.memset(start[:, NW:BINS], float(NT)))
                link(v.tensor_tensor(start[:, 0:NW], tiles_end[n][:, :], tiles_f[:, :], ALU.subtract))
                link(v.scalar_tensor_tensor(out=offset[:, :], in0=start[:, :], scalar=float(P),
                                            in1=before[:, :], op0=ALU.mult, op1=ALU.add))
                link(v.tensor_scalar(offset[:, :], offset[:, :], -1.0, None, ALU.add))
                link(v.tensor_tensor(offset[:, 1:BINS], offset[:, 1:BINS], count3[:, 0:BINS - 1, COLS - 1],
                                     ALU.subtract))

            def place_in_bins(n):
                many(BINS, lambda b: v.scalar_tensor_tensor(
                    out=count3[:, b, :], in0=count3[:, b, :], scalar=offset[:, b:b + 1],
                    in1=onehot_hi[n][:, b, :], op0=ALU.add, op1=ALU.mult))

            def rows_of_list(row):
                link(v.tensor_copy(posi[:, :], posf[:, :]))
                link(v.tensor_scalar(pos_lo[:, :], posi[:, :], P - 1, None, ALU.bitwise_and))
                link(v.tensor_scalar(posi[:, :], posi[:, :], 7, None, ALU.arith_shift_right))
                link(v.scalar_tensor_tensor(out=row[:, :], in0=pos_lo[:, :], scalar=float(LT), in1=posi[:, :],
                                            op0=ALU.mult, op1=ALU.add))

            def positions():
                link(v.tensor_reduce(posf[:, :], count3.rearrange("p b t -> p t b"), AX.X, ALU.add))

            def find_windows(n, tile_map):
                link(v.tensor_tensor(end_diag[:, :], tiles_end[n][0:NW, :], keep.ident[0:NW, 0:NW], ALU.mult))
                link(v.tensor_reduce(end_col[:, :], end_diag[:, :], AX.X, ALU.add))
                v.tensor_scalar(ended, tile_nof[0:NW - 1, :], end_col[0:NW - 1, 0:1], None, ALU.is_ge
                                ).then_inc(end_ready, 1)
                dve.wait_ge(map_done, n + 1)
                link(v.tensor_copy(tile_map[:, :], pT[n][0:1, 0:NT]))

            dve.wait_ge(keys_in, 64)
            find_bins(0)
            count_bins(0, 0, BINS)
            total_bins(0)
            start_bins(0)
            place_in_bins(0)
            positions()
            rows_of_list(row_src)

            def layer_norm():
                dve.wait_ge(x_in, 32)
                many(NW, lambda w: v.bn_stats(stats[:, w, :], keep.resid[:, w, :]))
                many(NW, lambda w: v.bn_aggr(mv[:, w, :], stats[:, w, :]))
                v.tensor_scalar(std[:, :], mv[:, :, 1], EPS, None, ALU.add).then_inc(var_ready, 1)
                dve.wait_ge(std_ready, 1)
                v.reciprocal(rstd[:, :], std[:, :]).then_inc(ln_ready, 1)
                dve.wait_ge(ln_ready, 1)
                v.scalar_tensor_tensor(out=nmr[:, :], in0=mv[:, :, 0], scalar=-1.0, in1=rstd[:, :],
                                       op0=ALU.mult, op1=ALU.mult).then_inc(ln_ready, 1)
                dve.wait_ge(w_in, 48)
                link(v.tensor_copy(we_part[0][:, :], we[:, :]))
                link(v.tensor_tensor(we_r[:, :], we[:, :], we_part[0][:, :], ALU.subtract))
                link(v.tensor_copy(we_part[1][:, :], we_r[:, :]))
                v.tensor_tensor(we_part[2][:, :], we_r[:, :], we_part[1][:, :], ALU.subtract).then_inc(we_parts, 1)

            def pack_rows(i, j):
                s = 2 * i + j
                dve.wait_ge(feat_in[j], 16 * (i + 1))
                for c in range(2):
                    if not isinstance(i, int) or s > 0:
                        dve.wait_ge(scattered[c], (16 * CH) * s)
                    done = s * 14 + 7 * c
                    t0 = (2 * s + c) * CH
                    e = feat[:, j, c * CH:(c + 1) * CH, :]
                    f16 = ring16[:, c, :, :]
                    hi3 = f16[:, :, 4:4 + 3 * EF].rearrange("p t (r f) -> p t r f", r=3)
                    mid2 = f16[:, :, 4 + 3 * EF:4 + 5 * EF].rearrange("p t (r f) -> p t r f", r=2)
                    v.tensor_copy(hi3, e.unsqueeze(2).to_broadcast([P, CH, 3, EF])).then_inc(payload, 1)
                    v.tensor_copy(ring[:, c, :, 0], lo16[0][:, bass.ds(t0, CH)]).then_inc(payload, 1)
                    v.tensor_copy(ring_i[:, c, :, 1], key[1][:, bass.ds(t0, CH)]).then_inc(payload, 1)
                    v.tensor_copy(ring_row[:, c, :], row_src[:, bass.ds(t0, CH)]).then_inc(payload, 1)
                    dve.wait_ge(payload, done + 4)
                    v.tensor_tensor(rest[:, c, :, :], e, f16[:, :, 4:4 + EF], ALU.subtract).then_inc(payload, 1)
                    dve.wait_ge(payload, done + 5)
                    v.tensor_copy(mid2, rest[:, c, :, :].unsqueeze(2).to_broadcast([P, CH, 2, EF])
                                  ).then_inc(payload, 1)
                    dve.wait_ge(payload, done + 6)
                    v.tensor_tensor(f16[:, :, 4 + 5 * EF:4 + 6 * EF], rest[:, c, :, :],
                                    f16[:, :, 4 + 3 * EF:4 + 4 * EF], ALU.subtract).then_inc(payload, 1)

            def destination_list(s):
                if s == 0:
                    find_bins(1)
                elif s == 1:
                    count_bins(1, 0, BINS // 2)
                elif s == 2:
                    count_bins(1, BINS // 2, BINS)
                    total_bins(1)
                elif s == PLACE:
                    start_bins(1)
                    place_in_bins(1)
                elif s == PLACE + 1:
                    positions()
                elif s == PLACE + 2:
                    rows_of_list(keep.row_dst)
                    dve.wait_ge(filled, 16 * (LT // FR + 1))
                    link(v.tensor_copy(keep.pair_i[:, :, 0], key[0][:, :]))
                    link(v.tensor_copy(keep.pair[:, :, 1], lo16[1][:, :]))

            def step(i, j):
                s = 2 * i + j
                pack_rows(i, j)
                if isinstance(i, int) and s == 0:
                    layer_norm()
                if isinstance(i, int):
                    destination_list(s)
                for c in range(2):
                    for n in range(2):
                        k = 2 * c + n
                        if not isinstance(i, int) or s > 0:
                            dve.wait_ge(hist_done, 4 * s + k - 3)
                        lo = lo16[n][:, bass.ds((2 * s + c) * CH, CH)]
                        v.tensor_tensor(onehot_lo[:, k, :, :], lo.unsqueeze(2).to_broadcast([P, CH, P]),
                                        keep.iota16[:, :].unsqueeze(1).to_broadcast([P, CH, P]), ALU.is_equal
                                        ).then_inc(oh_ready, 1)
                if inside(i, j - 1, 2, NW):
                    dve.wait_ge(h_ready, s)
                    r = keep.resid[:, bass.ds(s - 1, 1), :].rearrange("p w d -> p (w d)")
                    v.tensor_tensor(r, r, h[:, (j - 1) % 2, :], ALU.add).then_inc(resid_done, 1)
                if inside(i, j - 2, 2, NW):
                    dve.wait_ge(ab_done, s - 1)
                    v.tensor_tensor(vA[:, :], pA[j][:, :], b1[:, :], ALU.add).then_inc(va_ready, 1)
                    dve.wait_ge(a_hi, s - 1)
                    if not isinstance(i, int) or s > 2:
                        dve.wait_ge(a_mid, s - 2)
                    v.tensor_tensor(rA[:, :], vA[:, :], a_part(s - 2, 0), ALU.subtract
                                    ).then_inc(ra_ready, 1)
                    dve.wait_ge(a_mid, s - 1)
                    v.tensor_tensor(a_part(s - 2, 2), rA[:, :],
                                    a_part(s - 2, 1), ALU.subtract).then_inc(a_lo, 1)

            walk(dve, step)
            find_windows(0, keep.src_map)
            find_windows(1, keep.dst_map)
            dve.wait_ge(hist_done, 4 * HALVES)
            v.tensor_copy(keep.deg_src[:, :], pH[0][:, 0:NW]).then_inc(deg_ready, 1)
            v.tensor_scalar(keep.dis[:, :], pH[1][:, 0:NW], 1.0, None, ALU.add).then_inc(deg_ready, 1)
            dve.wait_ge(sq_ready, 1)
            link(v.reciprocal(keep.dis[:, :], keep.dis[:, :]))

        @block.tensor
        def _(pe):
            mm = nc.tensor.matmul
            pe.wait_ge(consts, 6)
            def sums(n):
                pe.wait_ge(tot_ready, n + 1)
                mm(sum_before, before_m[:, :], tot[:, :], start=True, stop=True)
                mm(sum_all, ones[:, :], tot[:, :], start=True, stop=True).then_inc(sums_done, 1)
                pe.wait_ge(sums_used, n + 1)

            sums(0)

            def step(i, j):
                s = 2 * i + j
                if inside(i, j, 2, NW):
                    pe.wait_ge(h_ready, s + 1)
                    if not isinstance(i, int) or s >= 2:
                        pe.wait_ge(ht_ready, s - 1)
                    if isinstance(i, int) and s == PLACE:
                        sums(1)
                    for k in range(2):
                        last = nc.tensor.transpose(pT[j][:, k * P:(k + 1) * P], h[:, j, k * P:(k + 1) * P],
                                                   keep.ident[:, :])
                    last.then_inc(trh_done, 1)
                if inside(i, j - 1, 2, NW):
                    b = (j - 1) % 2
                    pe.wait_ge(ht_ready, s)
                    if not isinstance(i, int) or s >= 3:
                        pe.wait_ge(va_ready, s - 2)
                        pe.wait_ge(b_ready, s - 2)
                    if isinstance(i, int) and s == 1:
                        pe.wait_ge(w_in, 48)
                    for out, k0 in ((pA[b], 0), (pB[b], 2)):
                        for k in range(2):
                            last = mm(out[:, :], hT[:, b, k * P:(k + 1) * P], w1[:, k0 + k, :],
                                      start=(k == 0), stop=(k == 1))
                    last.then_inc(ab_done, 1)
                for c in range(2):
                    for n in range(2):
                        pe.wait_ge(oh_ready, 4 * s + 2 * c + n + 1)
                        for t in range(CH):
                            first = isinstance(i, int) and s == 0 and c == 0 and t == 0
                            end = isinstance(i, int) and s == HALVES - 1 and c == 1 and t == CH - 1
                            rhs = onehot_hi[n][:, 0:NW, bass.ds((2 * s + c) * CH + t, 1)].rearrange("p b t -> p (b t)")
                            last = mm(pH[n][:, 0:NW], onehot_lo[:, 2 * c + n, t, :], rhs, start=first, stop=end,
                                      skip_group_check=True)
                        last.then_inc(hist_done, 1)

            walk(pe, step)
            for n in range(2):
                pe.wait_ge(end_ready, n + 1)
                if n == 0:
                    pe.wait_ge(ht_ready, NW)
                mm(pT[n][:, 0:NT], ones[0:NW - 1, :], ended, start=True, stop=True).then_inc(map_done, 1)


class PairRing:

    def __init__(self, g, name):
        self.pair = g.sb(f"d_pair_{name}", [P, 2, LC, 2])
        self.row = g.sb(f"d_row_{name}", [P, 2, LC], I32)
        self.copied = g.sem(f"d_copied_{name}")
        self.out = [g.sem(f"d_out_{name}_{n}") for n in range(2)]


def scatter_pairs(nc, pool, dr, keep, ring, turn, i, k, col0):
    c = k // LC
    if k % LC == 0:
        if not isinstance(i, int) or i > 0:
            pool.wait_ge(ring.out[c], 16 * LC * i)
            hold(pool, turn)
        nc.gpsimd.tensor_copy(ring.pair[:, c, :, :].rearrange("p t w -> p (t w)"),
                              keep.pair_flat[:, bass.ds(2 * (col0 + k), 2 * LC)]).then_inc(ring.copied, 1)
        nc.gpsimd.tensor_copy(ring.row[:, c, :], keep.row_dst[:, bass.ds(col0 + k, LC)]).then_inc(ring.copied, 1)
        pool.wait_ge(ring.copied, 4 * i + 2 * c + 2)
        hold(pool, turn)
    nc.gpsimd.indirect_dma_start(
        dr.dst_list[:, :, :].rearrange("p t w -> (p t) w"),
        bass.IndirectOffsetOnAxis(ap=ring.row[:, c, k % LC:k % LC + 1], axis=0),
        ring.pair[:, c, k % LC, :], None).then_inc(ring.out[c], 16)


def edge_mlp(nc, io, dr, keep):
    with ExitStack() as stack:
        g = Names(nc, stack)
        S = keep.S
        T = 16
        LCS = T // LC
        rows = g.sb("rows", [P, LCS, LC, ROW])
        BR = 8
        rows_i = rows[:, :, :, :].rearrange("p s t w -> p (s t w)").bitcast(I32).rearrange(
            "p (s t w) -> p s t w", s=LCS, t=LC)
        rows16 = rows[:, :, :, :].rearrange("p s t w -> p (s t w)").bitcast(BF16).rearrange(
            "p (s t w) -> p s t w", s=LCS, t=LC)
        brow = g.sb("brow", [P, BR, HID])
        oh16 = g.sb("oh16", [P, 4, P], BF16)
        oh32 = g.sb("oh32", [P, 4, P])
        turned = g.sb("turned", [P, 2, 2 * P], BF16)
        pre = g.sb("pre", [P, 2, HID])
        hid = g.sb("hid", [P, 2, HID])
        pairs = PairRing(g, "edge")
        pT = [g.ps(f"pTurn{n}", [P, 2 * HID], BF16) for n in range(2)]
        pE = [g.ps(f"pEdge{n}", [P, HID]) for n in range(2)]
        pN = [g.ps(f"pNode{n}", [P, HID]) for n in range(2)]

        s_zero = g.sem("s_zero")
        rows_in = [g.sem(f"rows_in{n}") for n in range(LCS)]
        b_in = [g.sem(f"b_in{n}") for n in range(BR)]
        oh_ready = g.sem("oh_ready2")
        turn_done = g.sem("turn_done")
        turn_copied = g.sem("turn_copied")
        edge_done = g.sem("edge_done")
        pre_ready = g.sem("pre_ready")
        hid_ready = g.sem("hid_ready")
        node_done = g.sem("node_done")
        s_added = g.sem("s_added")
        LAST = NT // T - 1

        block = stack.enter_context(nc.Block())

        @block.sync
        def _(sp):
            def step(i, j):
                if j % LC:
                    return
                b = j // LC
                if not isinstance(i, int) or i > 0:
                    sp.wait_ge(pre_ready, T * i + j + LC - T)
                sp.dma_start(rows[:, b, :, :], dr.src_list[:, bass.ds(T * i + j, LC), :]).then_inc(rows_in[b], 16)

            blocks(sp, NT, T, 1, LAST, step)

        @block.gpsimd
        def _(pool):
            turn = keep.turn

            def step(i, j):
                if j % LC == 0:
                    pool.wait_ge(rows_in[j // LC], 16 * (i + 1))
                if not isinstance(i, int) or i > 0 or j >= BR:
                    pool.wait_ge(pre_ready, T * i + j - BR + 1)
                hold(pool, turn)
                nc.gpsimd.indirect_dma_start(
                    brow[:, j % BR, :], None, dr.B,
                    bass.IndirectOffsetOnAxis(ap=rows_i[:, j // LC, j % LC, 1:2], axis=0)).then_inc(b_in[j % BR], 16)

            def turn_with_pairs(i):
                for j in range(T):
                    step(i + 1, j)
                    if j % 2:
                        scatter_pairs(nc, pool, dr, keep, pairs, turn, i, j // 2, 8 * i)

            for j in range(T):
                step(0, j)
            turn_with_pairs(0)
            with pool.Fori(1, NT // T - 1) as i:
                turn_with_pairs(i)
            for q in pairs.out:
                pool.wait_ge(q, 16 * LC * (NT // T - 1))

        @block.tensor
        def _(pe):
            mm = nc.tensor.matmul
            win = {}

            def step(i, j):
                t = T * i + j
                if j == 0:
                    win.clear()
                    win.update(windows(nc, pe, keep.src_map, i, 1, T))
                if inside(i, j, T, NT):
                    pe.wait_ge(oh_ready, 2 * t + 2)
                    if not isinstance(i, int) or t >= 2:
                        pe.wait_ge(turn_copied, t - 1)
                    nc.tensor.transpose(pT[j % 2][:, 0:P], oh16[:, j % 4, :], keep.ident16[:, :])
                    nc.tensor.transpose(pT[j % 2][0:EW, P:2 * P], rows16[:, j // LC, j % LC, 4:4 + EW],
                                        keep.ident16[:, :]).then_inc(turn_done, 1)
                if inside(i, j - 1, T, NT):
                    b = (j - 1) % 2
                    pe.wait_ge(turn_copied, t)
                    if not isinstance(i, int) or t >= 3:
                        pe.wait_ge(pre_ready, t - 2)
                    w = win[j]
                    mm(pE[b][:, :], turned[0:EW, b, P:2 * P], keep.we[:, :], start=True, stop=False)
                    for k in range(3):
                        last = mm(pE[b][:, :], turned[:, b, 0:P], keep.A[:, bass.ds(w * (3 * HID) + k * HID, HID)],
                                  start=False, stop=(k == 2))
                    last.then_inc(edge_done, 1)
                if inside(i, j - 2, T, NT):
                    pe.wait_ge(hid_ready, t - 1)
                    if not isinstance(i, int) or t >= 4:
                        pe.wait_ge(s_added, t - 3)
                    mm(pN[j % 2][:, :], oh32[:, (j - 2) % 4, :], hid[:, j % 2, :], start=True, stop=True
                       ).then_inc(node_done, 1)

            blocks(pe, NT + 2, T, 1, LAST, step)

        @block.scalar
        def _(act):
            def step(i, j):
                t = T * i + j
                if inside(i, j, T, NT):
                    act.wait_ge(turn_done, t + 1)
                    if not isinstance(i, int) or t >= 2:
                        act.wait_ge(edge_done, t - 1)
                    nc.scalar.copy(turned[:, j % 2, 0:P], pT[j % 2][:, 0:P])
                    nc.scalar.copy(turned[0:EW, j % 2, P:2 * P], pT[j % 2][0:EW, P:2 * P]).then_inc(turn_copied, 1)
                if inside(i, j - 1, T, NT):
                    b = (j - 1) % 2
                    act.wait_ge(pre_ready, t)
                    if not isinstance(i, int) or t >= 3:
                        act.wait_ge(node_done, t - 2)
                    nc.scalar.activation(hid[:, b, :], pre[:, b, :], ACT.Relu).then_inc(hid_ready, 1)

            blocks(act, NT + 1, T, 1, LAST, step)

        @block.vector
        def _(dve):
            v = nc.vector
            v.memset(S[:, :], 0.0).then_inc(s_zero, 1)
            dve.wait_ge(s_zero, 1)

            win = {}

            def step(i, j):
                t = T * i + j
                if j == 0:
                    win.clear()
                    win.update(windows(nc, dve, keep.src_map, i, 4, T))
                if inside(i, j - 4, T, NT):
                    dve.wait_ge(node_done, t - 3)
                    if not isinstance(i, int) or t > 4:
                        dve.wait_ge(s_added, t - 4)
                    sw = S[:, bass.ds(win[j] * HID, HID)]
                    v.tensor_tensor(sw, sw, pN[j % 2][:, :], ALU.add).then_inc(s_added, 1)
                if inside(i, j, T, NT):
                    if j % LC == 0:
                        dve.wait_ge(rows_in[j // LC], 16 * (i + 1))
                    lo = rows[:, j // LC, j % LC, 0:1]
                    v.tensor_scalar(oh16[:, j % 4, :], keep.iota16[:, :], lo, None, ALU.is_equal).then_inc(oh_ready, 1)
                    v.tensor_scalar(oh32[:, j % 4, :], keep.iota[:, :], lo, None, ALU.is_equal).then_inc(oh_ready, 1)
                if inside(i, j - 2, T, NT):
                    b = (j - 2) % 2
                    dve.wait_ge(edge_done, t - 1)
                    dve.wait_ge(b_in[(j - 2) % BR], 16 * (i * (T // BR) + (j - 2) // BR + 1))
                    if not isinstance(i, int) or t >= 4:
                        dve.wait_ge(hid_ready, t - 3)
                    v.tensor_tensor(pre[:, b, :], pE[b][:, :], brow[:, (j - 2) % BR, :], ALU.add
                                    ).then_inc(pre_ready, 1)

            blocks(dve, NT + 4, T, 1, LAST, step)
            dve.wait_ge(s_added, NT)


def node_mlp(nc, io, dr, keep):
    with ExitStack() as stack:
        g = Names(nc, stack)
        mw2 = g.sb("mw2", [P, 4, D])
        uw1 = g.sb("uw1", [P, 4, HID])
        uw2 = g.sb("uw2", [P, 4, D])
        mb2 = g.sb("mb2", [P, D])
        ub2 = g.sb("ub2", [P, D])
        ub1 = g.sb("ub1", [P, 4])
        hT = g.sb("hT3", [P, 2, D])
        pairs = PairRing(g, "node")
        turn = keep.turn
        s_win = g.sb("s_win", [P, 2, HID])
        sT = g.sb("sT", [P, 2, HID])
        agg = g.sb("agg", [P, 2, D])
        aggT = g.sb("aggT", [P, 2, D])
        uT = g.sb("uT", [P, 2, HID])
        xm = g.sb("xm", [P, D])
        stats = g.sb("stats3", [P, NW, 6])
        mv = g.sb("mv3", [P, NW, 2])
        std = g.sb("std3", [P, NW])
        pS = [g.ps(f"pS3_{n}", [P, HID]) for n in range(2)]
        pU = [g.ps(f"pU3_{n}", [P, HID]) for n in range(2)]
        pX = [g.ps(f"pX3_{n}", [P, HID]) for n in range(2)]
        pG = g.ps("pG3", [P, HID])
        pR = g.ps("pR3", [P, HID])

        w_in = g.sem("w_in3")
        h_in = [g.sem(f"h_in3_{n}") for n in range(2)]
        s_copied = g.sem("s_copied")
        st_done = g.sem("st_done")
        st_ready = g.sem("st_ready")
        agg_done = g.sem("agg_done")
        agg_ready = g.sem("agg_ready")
        at_done = g.sem("at_done")
        at_ready = g.sem("at_ready")
        u_done = g.sem("u_done")
        u_ready = g.sem("u_ready")
        x_done = g.sem("x_done")
        xm_ready = g.sem("xm_ready")
        x_ready = g.sem("x_ready")
        stat_ready = g.sem("stat_ready")
        own = g.sem("own3")
        var_ready = g.sem("var_ready3")
        std_ready = g.sem("std_ready3")

        def walk(eng, body):
            blocks(eng, NW + 4, 2, 3, NW // 2, body)

        block = stack.enter_context(nc.Block())

        @block.sync
        def _(sp):
            sp.dma_start(mw2[:, :, :], io["L0_gnn_mW2"].rearrange("(k p) n -> p k n", p=P)).then_inc(w_in, 16)
            sp.dma_start(mb2[:, :], io["L0_gnn_mb2"].partition_broadcast(P)).then_inc(w_in, 16)
            sp.dma_start(uw1[:, :, :], io["L0_gnn_uW1"].rearrange("(k p) n -> p k n", p=P)).then_inc(w_in, 16)
            sp.dma_start(uw2[:, :, :], io["L0_gnn_uW2"].rearrange("(k p) n -> p k n", p=P)).then_inc(w_in, 16)
            sp.dma_start(ub2[:, :], io["L0_gnn_ub2"].partition_broadcast(P)).then_inc(w_in, 16)
            for k in range(4):
                sp.dma_start(ub1[:, k:k + 1], io["L0_gnn_ub1"][k * P:(k + 1) * P].rearrange("(p o) -> p o", o=1)
                             ).then_inc(w_in, 16)

            def step(i, j):
                if inside(i, j, 2, NW):
                    s = 2 * i + j
                    if not isinstance(i, int) or s >= 2:
                        sp.wait_ge(u_done, s - 1)
                    sp.dma_start(hT[:, j, :], dr.hT[bass.ds(s, 1), :, :].rearrange("w p n -> p (w n)")
                                 ).then_inc(h_in[j], 16)

            walk(sp, step)

        @block.gpsimd
        def _(pool):
            first = 8 * (NT // 16 - 1)
            turns = (COLS - first) // 8
            for k in range(8):
                scatter_pairs(nc, pool, dr, keep, pairs, turn, 0, k, first)
            with pool.Fori(1, turns) as i:
                for k in range(8):
                    scatter_pairs(nc, pool, dr, keep, pairs, turn, i, k, 8 * i + first)
            for q in pairs.out:
                pool.wait_ge(q, 16 * LC * turns)

        @block.tensor
        def _(pe):
            mm = nc.tensor.matmul
            pe.wait_ge(w_in, 16 * 9)

            def step(i, j):
                s = 2 * i + j
                looped = not isinstance(i, int)
                if inside(i, j - 4, 2, NW):
                    pe.wait_ge(u_ready, 4 * (s - 3))
                    if looped or s >= 6:
                        pe.wait_ge(xm_ready, s - 5)
                    for k in range(4):
                        last = mm(pX[j][:, 0:D], uT[:, j, k * P:(k + 1) * P], uw2[:, k, :], start=(k == 0), stop=(k == 3))
                    last.then_inc(x_done, 1)
                if inside(i, j - 3, 2, NW):
                    b = (j - 3) % 2
                    pe.wait_ge(at_ready, s - 2)
                    pe.wait_ge(h_in[b], 16 * (i + (j - 3) // 2 + 1))
                    if looped or s >= 5:
                        pe.wait_ge(u_ready, 4 * (s - 4))
                    for m in range(4):
                        for k in range(4):
                            rhs = (hT if k < 2 else aggT)[:, b, (k % 2) * P:(k % 2 + 1) * P]
                            last = mm(pU[b][:, m * P:(m + 1) * P], uw1[:, k, m * P:(m + 1) * P], rhs,
                                      start=(k == 0), stop=(k == 3))
                    last.then_inc(u_done, 1)
                if inside(i, j - 2, 2, NW):
                    pe.wait_ge(agg_ready, s - 1)
                    if looped or s >= 3:
                        pe.wait_ge(at_ready, s - 2)
                    for k in range(2):
                        last = nc.tensor.transpose(pR[:, k * P:(k + 1) * P], agg[:, j, k * P:(k + 1) * P],
                                                   keep.ident[:, :])
                    last.then_inc(at_done, 1)
                if inside(i, j - 1, 2, NW):
                    b = (j - 1) % 2
                    pe.wait_ge(st_ready, s)
                    if looped or s >= 2:
                        pe.wait_ge(agg_ready, s - 1)
                    for k in range(4):
                        last = mm(pG[:, 0:D], sT[:, b, k * P:(k + 1) * P], mw2[:, k, :], start=(k == 0), stop=(k == 3))
                    last.then_inc(agg_done, 1)
                if inside(i, j, 2, NW):
                    pe.wait_ge(s_copied, s + 1)
                    if looped or s >= 2:
                        pe.wait_ge(st_ready, s - 1)
                    for k in range(4):
                        last = nc.tensor.transpose(pS[j][:, k * P:(k + 1) * P],
                                                   s_win[:, j, k * P:(k + 1) * P], keep.ident[:, :])
                    last.then_inc(st_done, 1)

            walk(pe, step)

        @block.scalar
        def _(act):
            def step(i, j):
                s = 2 * i + j
                looped = not isinstance(i, int)
                if inside(i, j - 3, 2, NW):
                    b = (j - 3) % 2
                    act.wait_ge(u_done, s - 2)
                    if looped or s >= 5:
                        act.wait_ge(x_done, s - 4)
                    for m in range(4):
                        nc.scalar.activation(uT[:, b, m * P:(m + 1) * P], pU[b][:, m * P:(m + 1) * P], ACT.Relu,
                                             bias=ub1[:, m:m + 1]).then_inc(u_ready, 1)
                if inside(i, j - 2, 2, NW):
                    act.wait_ge(at_done, s - 1)
                    if looped or s >= 4:
                        act.wait_ge(u_done, s - 3)
                    nc.scalar.copy(aggT[:, j, :], pR[:, 0:D]).then_inc(at_ready, 1)
                if inside(i, j, 2, NW):
                    act.wait_ge(st_done, s + 1)
                    if looped or s >= 2:
                        act.wait_ge(agg_done, s - 1)
                    nc.scalar.copy(sT[:, j, :], pS[j][:, :]).then_inc(st_ready, 1)

            act.wait_ge(w_in, 16 * 9)
            walk(act, step)
            act.wait_ge(var_ready, 1)
            nc.scalar.activation(std[:, :], std[:, :], ACT.Sqrt).then_inc(std_ready, 1)

        @block.vector
        def _(dve):
            v = nc.vector
            dve.wait_ge(w_in, 16 * 9)

            def step(i, j):
                s = 2 * i + j
                looped = not isinstance(i, int)
                if inside(i, j, 2, NW):
                    if looped or s >= 2:
                        dve.wait_ge(st_done, s - 1)
                    v.tensor_copy(s_win[:, j, :], keep.S[:, bass.ds(s * HID, HID)]).then_inc(s_copied, 1)
                if inside(i, j - 4, 2, NW):
                    dve.wait_ge(x_done, s - 3)
                    if looped or s >= 5:
                        dve.wait_ge(x_ready, s - 4)
                    r = keep.resid[:, bass.ds(s - 4, 1), :].rearrange("p w d -> p (w d)")
                    v.tensor_tensor(xm[:, :], pX[j][:, 0:D], ub2[:, :], ALU.add).then_inc(xm_ready, 1)
                    dve.wait_ge(xm_ready, s - 3)
                    v.tensor_tensor(r, r, xm[:, :], ALU.add).then_inc(x_ready, 1)
                    dve.wait_ge(x_ready, s - 3)
                    v.bn_stats(stats[:, bass.ds(s - 4, 1), :].rearrange("p w c -> p (w c)"), r).then_inc(stat_ready, 1)
                if inside(i, j - 1, 2, NW):
                    b = (j - 1) % 2
                    dve.wait_ge(agg_done, s)
                    if looped or s >= 3:
                        dve.wait_ge(at_done, s - 2)
                    v.scalar_tensor_tensor(out=agg[:, b, :], in0=mb2[:, :], scalar=keep.deg_src[:, bass.ds(s - 1, 1)],
                                           in1=pG[:, 0:D], op0=ALU.mult, op1=ALU.add).then_inc(agg_ready, 1)

            walk(dve, step)
            dve.wait_ge(stat_ready, NW)
            link = Chain(dve, own)
            for w in range(NW):
                link(v.bn_aggr(mv[:, w, :], stats[:, w, :]))
            v.tensor_scalar(std[:, :], mv[:, :, 1], EPS, None, ALU.add).then_inc(var_ready, 1)
            dve.wait_ge(std_ready, 1)
            link(v.reciprocal(keep.rstd[:, :], std[:, :]))
            link(v.scalar_tensor_tensor(out=keep.nmr[:, :], in0=mv[:, :, 0], scalar=-1.0, in1=keep.rstd[:, :],
                                        op0=ALU.mult, op1=ALU.mult))


def project(nc, io, dr, keep, layer):
    with ExitStack() as stack:
        g = Names(nc, stack)
        w = g.sb(f"w_{layer}", [P, 2, D])
        bias = g.sb(f"bias_{layer}", [P, D])
        z = g.sb(f"z_{layer}", [P, 2, D])
        if layer == 2:
            b3 = g.sb("b3", [P, D])
            b3_added = g.sem("b3_added")
        h = g.sb(f"h_{layer}", [P, 2, D])
        hT = g.sb(f"hT_{layer}", [P, 2, D])
        pT = [g.ps(f"pT_{layer}_{n}", [P, HID]) for n in range(2)]
        pY = [g.ps(f"pY_{layer}_{n}", [P, HID]) for n in range(2)]
        w_in = g.sem(f"w_in_{layer}")
        z_ready = g.sem(f"z_ready_{layer}")
        h_ready = g.sem(f"h_ready_{layer}")
        tr_done = g.sem(f"tr_done_{layer}")
        ht_ready = g.sem(f"ht_ready_{layer}")
        y_done = g.sem(f"y_done_{layer}")
        y_ready = g.sem(f"y_ready_{layer}")
        y_out = g.sem(f"y_out_{layer}")
        pairs_in = g.sem(f"pairs_in_{layer}")

        def walk(eng, body):
            blocks(eng, NW + 3, 2, 2, NW // 2, body)

        block = stack.enter_context(nc.Block())

        @block.sync
        def _(sp):
            sp.dma_start(w[:, :, :], io[f"L1_gnn_W{layer}"].rearrange("(k p) n -> p k n", p=P)).then_inc(w_in, 16)
            if layer > 1:
                sp.dma_start(bias[:, :], io[f"L1_gnn_b{layer - 1}"].partition_broadcast(P)).then_inc(w_in, 16)
                if layer == 2:
                    sp.dma_start(b3[:, :], io["L1_gnn_b3"].partition_broadcast(P)).then_inc(w_in, 16)
            else:
                sp.dma_start(keep.pairs[:, :, :], dr.dst_list[:, :, :]).then_inc(pairs_in, 16)

            def step(i, j):
                s = 2 * i + j
                if inside(i, j - 3, 2, NW):
                    sp.wait_ge(y_ready, s - 2)
                    sp.dma_start(dr.Y[bass.ds((s - 3) * P, P), :], keep.acc[:, bass.ds((s - 3) * D, D)]
                                 ).then_inc(y_out, 16)

            walk(sp, step)
            sp.wait_ge(y_out, 16 * NW)
            if layer == 1:
                sp.wait_ge(pairs_in, 16)

        @block.vector
        def _(dve):
            v = nc.vector
            dve.wait_ge(w_in, 16 * (1 + (layer > 1) + (layer == 2)))

            def step(i, j):
                s = 2 * i + j
                looped = not isinstance(i, int)
                if layer > 1 and inside(i, j, 2, NW):
                    if looped or s >= 2:
                        dve.wait_ge(h_ready, s - 1)
                    v.scalar_tensor_tensor(out=z[:, j, :], in0=keep.acc[:, bass.ds(s * D, D)],
                                           scalar=keep.dis[:, bass.ds(s, 1)], in1=bias[:, :],
                                           op0=ALU.mult, op1=ALU.add).then_inc(z_ready, 1)
                if layer == 2 and inside(i, j, 2, NW):
                    x = keep.resid[:, bass.ds(s, 1), :].rearrange("p w d -> p (w d)")
                    v.tensor_tensor(x, x, b3[:, :], ALU.add).then_inc(b3_added, 1)
                if inside(i, j - 3, 2, NW):
                    dve.wait_ge(y_done, s - 2)
                    v.tensor_scalar(keep.acc[:, bass.ds((s - 3) * D, D)], pY[(j - 3) % 2][:, 0:D],
                                    keep.dis[:, bass.ds(s - 3, 1)], None, ALU.mult).then_inc(y_ready, 1)

            walk(dve, step)

        @block.scalar
        def _(act):
            def step(i, j):
                s = 2 * i + j
                looped = not isinstance(i, int)
                if inside(i, j, 2, NW):
                    if looped or s >= 2:
                        act.wait_ge(tr_done, s - 1)
                    if layer == 1:
                        nc.scalar.activation(h[:, j, :], keep.resid[:, bass.ds(s, 1), :].rearrange("p w d -> p (w d)"),
                                             ACT.Relu, bias=keep.nmr[:, bass.ds(s, 1)],
                                             scale=keep.rstd[:, bass.ds(s, 1)]).then_inc(h_ready, 1)
                    else:
                        act.wait_ge(z_ready, s + 1)
                        nc.scalar.activation(h[:, j, :], z[:, j, :], ACT.Gelu_apprx_tanh).then_inc(h_ready, 1)
                if inside(i, j - 1, 2, NW):
                    b = (j - 1) % 2
                    act.wait_ge(tr_done, s)
                    if looped or s >= 3:
                        act.wait_ge(y_done, s - 2)
                    nc.scalar.copy(hT[:, b, :], pT[b][:, 0:D]).then_inc(ht_ready, 1)

            walk(act, step)

        @block.tensor
        def _(pe):
            pe.wait_ge(w_in, 16 * (1 + (layer > 1) + (layer == 2)))

            def step(i, j):
                s = 2 * i + j
                looped = not isinstance(i, int)
                if inside(i, j, 2, NW):
                    pe.wait_ge(h_ready, s + 1)
                    if looped or s >= 2:
                        pe.wait_ge(ht_ready, s - 1)
                    for k in range(2):
                        last = nc.tensor.transpose(pT[j][:, k * P:(k + 1) * P], h[:, j, k * P:(k + 1) * P],
                                                   keep.ident[:, :])
                    last.then_inc(tr_done, 1)
                if inside(i, j - 1, 2, NW):
                    b = (j - 1) % 2
                    pe.wait_ge(ht_ready, s)
                    if looped or s >= 3:
                        pe.wait_ge(y_ready, s - 2)
                    for k in range(2):
                        last = nc.tensor.matmul(pY[b][:, 0:D], hT[:, b, k * P:(k + 1) * P], w[:, k, :],
                                                start=(k == 0), stop=(k == 1))
                    last.then_inc(y_done, 1)

            walk(pe, step)


def spread(nc, io, dr, keep, layer):
    with ExitStack() as stack:
        g = Names(nc, stack)
        R = GATHERS
        rows = g.sb(f"rows_{layer}", [P, R, D])
        index = g.sb(f"index_{layer}", [P, R // 2, 2], I32)
        onehot = g.sb(f"onehot_{layer}", [P, R, P])
        pN = [g.ps(f"pN_{layer}_{n}", [P, HID]) for n in range(4)]
        index_ready = g.sem(f"index_ready_{layer}")
        oh_ready = g.sem(f"oh_ready_{layer}")
        rows_in = keep.rows_in
        before = 16 * (NT // R) * (layer - 1)
        node_done = g.sem(f"node_done_{layer}")
        added = g.sem(f"added_{layer}")
        pairs_i = keep.pairs_i
        LAST = NT // R - 1

        block = stack.enter_context(nc.Block())

        @block.gpsimd
        def _(pool):
            turn = keep.turn

            def step(i, j):
                t = R * i + j
                if j % 2 == 0:
                    pool.wait_ge(index_ready, (R // 2) * i + j // 2 + 1)
                if not isinstance(i, int) or t >= R:
                    pool.wait_ge(node_done, t - R + 1)
                hold(pool, turn)
                nc.gpsimd.indirect_dma_start(
                    rows[:, j, :], None, dr.Y,
                    bass.IndirectOffsetOnAxis(ap=index[:, j // 2, j % 2:j % 2 + 1], axis=0)).then_inc(rows_in[j], 16)

            blocks(pool, NT, R, 1, LAST, step)

        @block.tensor
        def _(pe):
            def step(i, j):
                t = R * i + j
                pe.wait_ge(oh_ready, t + 1)
                pe.wait_ge(rows_in[j], 16 * i + (16 + before))
                if not isinstance(i, int) or t >= 4:
                    pe.wait_ge(added, t - 3)
                nc.tensor.matmul(pN[j % 4][:, 0:D], onehot[:, j, :], rows[:, j, :], start=True, stop=True
                                 ).then_inc(node_done, 1)

            blocks(pe, NT, R, 1, LAST, step)

        @block.vector
        def _(dve):
            v = nc.vector

            win = {}

            def step(i, j):
                t = R * i + j
                if j == 0:
                    win.clear()
                    win.update(windows(nc, dve, keep.dst_map, i, R, R))
                if inside(i, j - R, R, NT):
                    dve.wait_ge(node_done, t - R + 1)
                    if not isinstance(i, int) or t > R:
                        dve.wait_ge(added, t - R)
                    sw = keep.acc[:, bass.ds(win[j] * D, D)]
                    v.tensor_tensor(sw, sw, pN[j % 4][:, 0:D], ALU.add).then_inc(added, 1)
                if inside(i, j, R, NT):
                    v.tensor_scalar(onehot[:, j, :], keep.iota[:, :], keep.pairs[:, bass.ds(t, 1), 1:2].rearrange(
                        "p t w -> p (t w)"), None, ALU.is_equal).then_inc(oh_ready, 1)
                    if j % 2:
                        v.tensor_copy(index[:, j // 2, :], pairs_i[:, bass.ds(t - 1, 2), 0]).then_inc(index_ready, 1)

            blocks(dve, NT + R, R, 2, NT // R, step)


def finish(nc, io, dr, keep, out):
    with ExitStack() as stack:
        g = Names(nc, stack)
        res = g.sem("res_out")
        stored = g.sem("stored")
        block = stack.enter_context(nc.Block())

        @block.sync
        def _(sp):
            for w in range(NW):
                sp.wait_ge(res, w + 1)
                n = P if w < NW - 1 else TAIL
                sp.dma_start(out[w * P:w * P + n, :], keep.resid[0:n, w, :]).then_inc(stored, 16)
            sp.wait_ge(stored, 16 * NW)

        @block.vector
        def _(dve):
            v = nc.vector
            for w in range(NW):
                r = keep.resid[:, w, :]
                v.scalar_tensor_tensor(out=r, in0=keep.acc[:, w * D:(w + 1) * D], scalar=keep.dis[:, w:w + 1], in1=r,
                                       op0=ALU.mult, op1=ALU.add).then_inc(res, 1)


class Store:
    pass


def build(nc, io, out):
    dr, keep = Store(), Store()
    with ExitStack() as stack:
        g = Names(nc, stack)
        dr.src_list = nc.dram_tensor("src_list", [P, LT, ROW], F32).ap()
        dr.dst_list = nc.dram_tensor("dst_list", [P, LT, 2], F32).ap()
        dr.feat = nc.dram_tensor("feat_rows", [COLS * P, EF], F32).ap()
        dr.hT = nc.dram_tensor("hT_rows", [NW, P, D], F32).ap()
        dr.B = nc.dram_tensor("B_rows", [NPAD, HID], F32).ap()
        dr.Y = nc.dram_tensor("Y_rows", [NPAD, D], F32).ap()
        keep.turn = g.sem("turn")
        keep.resid = g.sb("resid", [P, NW, D])
        keep.iota = g.sb("iota", [P, P])
        keep.iota16 = g.sb("iota16", [P, P], BF16)
        keep.ident = g.sb("ident", [P, P])
        keep.ident16 = g.sb("ident16", [P, P], BF16)
        keep.dis = g.sb("dis", [P, NW])
        keep.deg_src = g.sb("deg_src", [P, NW])
        keep.rstd = g.sb("rstd_k", [P, NW])
        keep.nmr = g.sb("nmr_k", [P, NW])
        keep.src_map = g.sb("src_map", [1, NT], I32)
        keep.dst_map = g.sb("dst_map", [1, NT], I32)
        with ExitStack() as inner:
            k = Names(nc, inner)
            keep.A = k.sb("A", [P, NW * 3 * HID], BF16)
            keep.row_dst = k.sb("row_dst", [P, COLS], I32)
            pair = k.sb("pair", [P, LT * 2])
            keep.pair_w = pair[:, :].rearrange("p (t w) -> p t w", w=2)
            keep.pair_flat = pair
            keep.pair = keep.pair_w[:, 0:COLS, :]
            keep.pair_i = pair[:, :].bitcast(I32).rearrange("p (t w) -> p t w", w=2)[:, 0:COLS, :]
            keep.we = k.sb("we_rows", [EW, HID], BF16)
            sort_and_embed(nc, io, dr, keep)
            with ExitStack() as high:
                keep.S = Names(nc, high).sb("S", [P, NW * HID])
                edge_mlp(nc, io, dr, keep)
                node_mlp(nc, io, dr, keep)
        keep.acc = g.sb("acc", [P, NW * D])
        pairs = g.sb("pairs", [P, LT * 2])
        keep.pairs = pairs[:, :].rearrange("p (t w) -> p t w", w=2)
        keep.pairs_i = pairs[:, :].bitcast(I32).rearrange("p (t w) -> p t w", w=2)
        keep.rows_in = [g.sem(f"y_rows_in_{n}") for n in range(GATHERS)]
        for layer in (1, 2, 3):
            project(nc, io, dr, keep, layer)
            spread(nc, io, dr, keep, layer)
        finish(nc, io, dr, keep, out)


_INS = ["x", "src", "dst", "edge_attr_16", "L0_gnn_mW1", "L0_gnn_mb1", "L0_gnn_mW2", "L0_gnn_mb2", "L0_gnn_uW1",
        "L0_gnn_ub1", "L0_gnn_uW2", "L0_gnn_ub2", "L1_gnn_W1", "L1_gnn_b1", "L1_gnn_W2", "L1_gnn_b2", "L1_gnn_W3",
        "L1_gnn_b3"]


def kernel(**inputs):
    import numpy as _np
    import concourse.bacc as _bacc
    from concourse import mybir as _mybir
    from concourse.bass_utils import run_bass_kernel_spmd as _run

    nc = _bacc.Bacc("TRN2", target_bir_lowering=False, num_devices=1)
    arrays, io = {}, {}
    for name in _INS:
        a = _np.ascontiguousarray(inputs[name])
        arrays[f"in_{name}_dram"] = a
        io[name] = nc.dram_tensor(f"in_{name}_dram", a.shape, _mybir.dt.from_np(a.dtype), kind="ExternalInput").ap()
    out = nc.dram_tensor("out_0_dram", (N, D), _mybir.dt.float32, kind="ExternalOutput").ap()
    build(nc, io, out)
    r = _run(nc, [arrays], core_ids=[0])
    return r.results[0]["out_0_dram"]
```
